# Optimizing a Trainium2 kernel written in Bass

```python
import numpy as np
import jax
import jax.numpy as jnp

def _softmax(x, axis=-1):
    return jax.nn.softmax(x, axis=axis)

def _gelu(x):
    return jax.nn.gelu(x, approximate=True)

def _silu(x):
    return jax.nn.silu(x)

def _sigmoid(x):
    return jax.nn.sigmoid(x)

def _layernorm(x, axis=-1, eps=1e-05):
    m = jnp.mean(x, axis=axis, keepdims=True)
    v = jnp.var(x, axis=axis, keepdims=True)
    return (x - m) / jnp.sqrt(v + eps)

def _scatter_add(tgt, idx, src, axis=0):
    return tgt.at[idx].add(src)

def _segment_sum(src, seg, n):
    return jax.ops.segment_sum(src, seg, n)
kernel_name = 'mk_prb_d2_jaxref_r8_bff95b'

def setup_inputs(seed: int=0):
    np.random.seed(seed)
    _w = jnp.asarray

    def _L0_attn_setup():
        import jax, jax.numpy as jnp
        import numpy as np
        N_HEADS = 16
        EPS = 0.0001

        def _cosformer(x, Wq, bq, Wk, bk, Wv, bv, Wo, bo):
            B, L, E = x.shape
            H = N_HEADS
            hd = E // H
            q = jax.nn.relu(jnp.einsum('ble,fe->blf', x, Wq) + bq)
            k = jax.nn.relu(jnp.einsum('ble,fe->blf', x, Wk) + bk)
            v = jnp.einsum('ble,fe->blf', x, Wv) + bv

            def split_heads(t):
                return t.reshape(B, L, H, hd).transpose(0, 2, 1, 3).reshape(B * H, L, hd)
            q, k, v = (split_heads(q), split_heads(k), split_heads(v))
            m = L
            idx = np.pi / 2 * jnp.arange(1, m + 1, dtype=jnp.float32) / m
            sin = jnp.sin(idx)[None, :, None]
            cos = jnp.cos(idx)[None, :, None]
            q_ = jnp.concatenate([q * sin, q * cos], axis=-1)
            k_ = jnp.concatenate([k * sin, k * cos], axis=-1)
            kv = jnp.einsum('nld,nlm->ndm', k_, v)
            z = 1.0 / jnp.maximum(jnp.einsum('nld,nd->nl', q_, k_.sum(axis=1)), EPS)
            attn = jnp.einsum('nld,ndm->nlm', q_, kv) * z[:, :, None]
            out = attn.reshape(B, H, L, hd).transpose(0, 2, 1, 3).reshape(B, L, E)
            return jnp.einsum('ble,fe->blf', out, Wo) + bo
        key = jax.random.key(seed)
        ks = jax.random.split(key, 9)
        B, L, E = (4, 512, 128)
        s = 1.0 / np.sqrt(E)
        return {'x': jax.random.normal(ks[0], (B, L, E), dtype=jnp.float32), 'Wq': jax.random.normal(ks[1], (E, E), dtype=jnp.float32) * s, 'bq': jax.random.normal(ks[2], (E,), dtype=jnp.float32) * 0.01, 'Wk': jax.random.normal(ks[3], (E, E), dtype=jnp.float32) * s, 'bk': jax.random.normal(ks[4], (E,), dtype=jnp.float32) * 0.01, 'Wv': jax.random.normal(ks[5], (E, E), dtype=jnp.float32) * s, 'bv': jax.random.normal(ks[6], (E,), dtype=jnp.float32) * 0.01, 'Wo': jax.random.normal(ks[7], (E, E), dtype=jnp.float32) * s, 'bo': jax.random.normal(ks[8], (E,), dtype=jnp.float32) * 0.01}
    _L0_attn_in = _L0_attn_setup()

    def _L0_ffn_setup():
        import jax, jax.numpy as jnp
        import numpy as np
        H_DIM, E_DIM = (128, 64)
        N_SHARED, N_ROUTED, TOP_K = (2, 16, 4)
        B, S = (4, 256)
        key = jax.random.key(seed)
        ks = jax.random.split(key, 6)
        sc = 1.0 / np.sqrt(H_DIM)
        ec = 1.0 / np.sqrt(E_DIM)
        return {'x': jax.random.normal(ks[0], (B, S, H_DIM), dtype=jnp.float32), 'shared_up': jax.random.uniform(ks[1], (N_SHARED, E_DIM, H_DIM), jnp.float32, -sc, sc), 'shared_down': jax.random.uniform(ks[2], (N_SHARED, H_DIM, E_DIM), jnp.float32, -ec, ec), 'routed_up': jax.random.uniform(ks[3], (N_ROUTED, E_DIM, H_DIM), jnp.float32, -sc, sc), 'routed_down': jax.random.uniform(ks[4], (N_ROUTED, H_DIM, E_DIM), jnp.float32, -ec, ec), 'router_w': jax.random.uniform(ks[5], (N_ROUTED, H_DIM), jnp.float32, -sc, sc)}
    _L0_ffn_in = _L0_ffn_setup()

    def _L1_attn_setup():
        import jax, jax.numpy as jnp
        import numpy as np
        D_MODEL = 128
        N_HEADS = 16

        def get_freqs(seq, n_dim):
            inv = 1.0 / 10000.0 ** (jnp.arange(0, n_dim, 2, dtype=jnp.float32) / n_dim)
            pos = jnp.arange(seq, dtype=jnp.float32)
            return pos[:, None] * inv[None, :]

        def rope(x, freq):
            xf = x.astype(jnp.float32)
            x1 = xf[..., 0::2]
            x2 = xf[..., 1::2]
            cos = jnp.cos(freq)[None, :, None, :]
            sin = jnp.sin(freq)[None, :, None, :]
            r1 = x1 * cos - x2 * sin
            r2 = x1 * sin + x2 * cos
            out = jnp.stack([r1, r2], axis=-1).reshape(x.shape)
            return out.astype(x.dtype)
        key = jax.random.key(seed)
        k1, k2, k3, k4, k5 = jax.random.split(key, 5)
        batch, seq = (2, 256)
        x = jax.random.normal(k1, (batch, seq, D_MODEL), dtype=jnp.float16)
        scale = jnp.float16(0.02)
        qw = jax.random.normal(k2, (D_MODEL, D_MODEL), dtype=jnp.float16) * scale
        kw = jax.random.normal(k3, (D_MODEL, D_MODEL), dtype=jnp.float16) * scale
        vw = jax.random.normal(k4, (D_MODEL, D_MODEL), dtype=jnp.float16) * scale
        ow = jax.random.normal(k5, (D_MODEL, D_MODEL), dtype=jnp.float16) * scale
        return {'x': x, 'qw': qw, 'kw': kw, 'vw': vw, 'ow': ow}
    _L1_attn_in = _L1_attn_setup()

    def _L1_ffn_setup():
        import jax, jax.numpy as jnp
        import numpy as np
        B, S, DIM, FFN, E = (4, 256, 128, 512, 8)
        key = jax.random.key(seed)
        k0, k1, k2, k3 = jax.random.split(key, 4)
        scale = 0.02
        return {'hidden_states': jax.random.normal(k0, (B, S, DIM), jnp.float32), 'router_w': jax.random.normal(k1, (DIM, E), jnp.float32) * scale, 'router_b': jnp.zeros((E,), jnp.float32), 'w1': jax.random.normal(k2, (E, DIM, 2 * FFN), jnp.float32) * scale, 'w2': jax.random.normal(k3, (E, FFN, DIM), jnp.float32) * scale}
    _L1_ffn_in = _L1_ffn_setup()
    _d = {'L0_attn_x': _L0_attn_in['x'], 'L0_attn_Wq': _L0_attn_in['Wq'], 'L0_attn_bq': _L0_attn_in['bq'], 'L0_attn_Wk': _L0_attn_in['Wk'], 'L0_attn_bk': _L0_attn_in['bk'], 'L0_attn_Wv': _L0_attn_in['Wv'], 'L0_attn_bv': _L0_attn_in['bv'], 'L0_attn_Wo': _L0_attn_in['Wo'], 'L0_attn_bo': _L0_attn_in['bo'], 'L0_ffn_shared_up': _L0_ffn_in['shared_up'], 'L0_ffn_shared_down': _L0_ffn_in['shared_down'], 'L0_ffn_routed_up': _L0_ffn_in['routed_up'], 'L0_ffn_routed_down': _L0_ffn_in['routed_down'], 'L0_ffn_router_w': _L0_ffn_in['router_w'], 'L1_attn_qw': _L1_attn_in['qw'], 'L1_attn_kw': _L1_attn_in['kw'], 'L1_attn_vw': _L1_attn_in['vw'], 'L1_attn_ow': _L1_attn_in['ow'], 'L1_ffn_router_w': _L1_ffn_in['router_w'], 'L1_ffn_router_b': _L1_ffn_in['router_b'], 'L1_ffn_w1': _L1_ffn_in['w1'], 'L1_ffn_w2': _L1_ffn_in['w2']}
    _x0 = _d['L0_attn_x']
    _d['L0_attn_x'] = jax.random.normal(jax.random.fold_in(jax.random.key(seed), 1), (16, 512, 128), dtype=_x0.dtype)
    del _x0
    return _d

def reference(L0_attn_x, L0_attn_Wq, L0_attn_bq, L0_attn_Wk, L0_attn_bk, L0_attn_Wv, L0_attn_bv, L0_attn_Wo, L0_attn_bo, L0_ffn_shared_up, L0_ffn_shared_down, L0_ffn_routed_up, L0_ffn_routed_down, L0_ffn_router_w, L1_attn_qw, L1_attn_kw, L1_attn_vw, L1_attn_ow, L1_ffn_router_w, L1_ffn_router_b, L1_ffn_w1, L1_ffn_w2):

    def _L0_attn_ref(x, Wq, bq, Wk, bk, Wv, bv, Wo, bo):
        import jax, jax.numpy as jnp
        import numpy as np
        N_HEADS = 16
        EPS = 0.0001

        def _cosformer(x, Wq, bq, Wk, bk, Wv, bv, Wo, bo):
            B, L, E = x.shape
            H = N_HEADS
            hd = E // H
            q = jax.nn.relu(jnp.einsum('ble,fe->blf', x, Wq) + bq)
            k = jax.nn.relu(jnp.einsum('ble,fe->blf', x, Wk) + bk)
            v = jnp.einsum('ble,fe->blf', x, Wv) + bv

            def split_heads(t):
                return t.reshape(B, L, H, hd).transpose(0, 2, 1, 3).reshape(B * H, L, hd)
            q, k, v = (split_heads(q), split_heads(k), split_heads(v))
            m = L
            idx = np.pi / 2 * jnp.arange(1, m + 1, dtype=jnp.float32) / m
            sin = jnp.sin(idx)[None, :, None]
            cos = jnp.cos(idx)[None, :, None]
            q_ = jnp.concatenate([q * sin, q * cos], axis=-1)
            k_ = jnp.concatenate([k * sin, k * cos], axis=-1)
            kv = jnp.einsum('nld,nlm->ndm', k_, v)
            z = 1.0 / jnp.maximum(jnp.einsum('nld,nd->nl', q_, k_.sum(axis=1)), EPS)
            attn = jnp.einsum('nld,ndm->nlm', q_, kv) * z[:, :, None]
            out = attn.reshape(B, H, L, hd).transpose(0, 2, 1, 3).reshape(B, L, E)
            return jnp.einsum('ble,fe->blf', out, Wo) + bo
        return _cosformer(x, Wq, bq, Wk, bk, Wv, bv, Wo, bo)

    def _L0_ffn_ref(x, shared_up, shared_down, routed_up, routed_down, router_w):
        import jax, jax.numpy as jnp
        import numpy as np
        H_DIM, E_DIM = (128, 64)
        N_SHARED, N_ROUTED, TOP_K = (2, 16, 4)
        B, S = (4, 256)
        b, s, h = x.shape
        xt = x.reshape(-1, h)
        up_s = jnp.einsum('th,seh->tse', xt, shared_up)
        shared = jnp.einsum('tse,she->th', jax.nn.gelu(up_s, approximate=False), shared_down)
        probs = jax.nn.softmax(xt @ router_w.T, axis=-1)
        topk_p, topk_i = jax.lax.top_k(probs, TOP_K)
        gate = jnp.zeros_like(probs).at[jnp.arange(xt.shape[0])[:, None], topk_i].add(topk_p)
        up_r = jnp.einsum('th,reh->tre', xt, routed_up)
        act = jax.nn.gelu(up_r, approximate=False) * gate[:, :, None]
        routed = jnp.einsum('tre,rhe->th', act, routed_down)
        return (shared + routed).reshape(b, s, h)

    def _L1_attn_ref(x, qw, kw, vw, ow):
        import jax, jax.numpy as jnp
        import numpy as np
        D_MODEL = 128
        N_HEADS = 16

        def get_freqs(seq, n_dim):
            inv = 1.0 / 10000.0 ** (jnp.arange(0, n_dim, 2, dtype=jnp.float32) / n_dim)
            pos = jnp.arange(seq, dtype=jnp.float32)
            return pos[:, None] * inv[None, :]

        def rope(x, freq):
            xf = x.astype(jnp.float32)
            x1 = xf[..., 0::2]
            x2 = xf[..., 1::2]
            cos = jnp.cos(freq)[None, :, None, :]
            sin = jnp.sin(freq)[None, :, None, :]
            r1 = x1 * cos - x2 * sin
            r2 = x1 * sin + x2 * cos
            out = jnp.stack([r1, r2], axis=-1).reshape(x.shape)
            return out.astype(x.dtype)
        batch, seq, dim = x.shape
        n_heads = N_HEADS
        n_dim = dim // n_heads
        Q = (x @ qw).reshape(batch, seq, n_heads, n_dim)
        K = (x @ kw).reshape(batch, seq, n_heads, n_dim)
        V = (x @ vw).reshape(batch, seq, n_heads, n_dim)
        freq = get_freqs(seq, n_dim)
        Q = rope(Q, freq)
        K = rope(K, freq)
        Q = jnp.transpose(Q, (0, 2, 1, 3))
        K = jnp.transpose(K, (0, 2, 1, 3))
        V = jnp.transpose(V, (0, 2, 1, 3))
        score = Q @ jnp.swapaxes(K, -1, -2) / jnp.sqrt(jnp.float16(dim))
        score = score.astype(jnp.float32)
        mask = jnp.tril(jnp.ones((1, 1, seq, seq), dtype=jnp.float32))
        score = score - 10000000000.0 * (1.0 - mask)
        weights = jax.nn.softmax(score, axis=-1)
        attn = weights @ V.astype(jnp.float32)
        merged = jnp.transpose(attn, (0, 2, 1, 3)).reshape(batch, seq, dim)
        out = merged @ ow.astype(jnp.float32)
        return out

    def _L1_ffn_ref(hidden_states, router_w, router_b, w1, w2):
        import jax, jax.numpy as jnp
        import numpy as np
        B, S, DIM, FFN, E = (4, 256, 128, 512, 8)
        b, s, d = hidden_states.shape
        x = hidden_states.reshape(-1, d)
        logits = x @ router_w + router_b
        route = jax.nn.softmax(logits, axis=1)
        max_prob = jnp.max(route, axis=1, keepdims=True)
        max_ind = jnp.argmax(route, axis=1)
        out = jnp.zeros_like(x)
        num_experts = w1.shape[0]
        for e in range(num_experts):
            h = x @ w1[e]
            a, g = jnp.split(h, 2, axis=1)
            y = jax.nn.silu(a) * g @ w2[e]
            out = jnp.where((max_ind == e)[:, None], y, out)
        out = out * max_prob
        return out.reshape(b, s, d)
    x = L0_attn_x
    xn = _layernorm(x, axis=-1)
    x = x + _L0_attn_ref(xn, L0_attn_Wq, L0_attn_bq, L0_attn_Wk, L0_attn_bk, L0_attn_Wv, L0_attn_bv, L0_attn_Wo, L0_attn_bo) + _L0_ffn_ref(xn, L0_ffn_shared_up, L0_ffn_shared_down, L0_ffn_routed_up, L0_ffn_routed_down, L0_ffn_router_w)
    xn = _layernorm(x, axis=-1)
    x = x + _L1_attn_ref(xn, L1_attn_qw, L1_attn_kw, L1_attn_vw, L1_attn_ow) + _L1_ffn_ref(xn, L1_ffn_router_w, L1_ffn_router_b, L1_ffn_w1, L1_ffn_w2)
    return x

_drawn_inputs = setup_inputs


def setup_inputs(seed=0):
    import zlib

    import numpy as np

    out = dict(_drawn_inputs(seed))
    spreads = {'L1_ffn_router_b': (0.0, 0.8)}
    factors = {'L0_attn_bq': 8.0,
     'L0_attn_bk': 8.0,
     'L0_attn_bv': 5.481,
     'L0_attn_bo': 5.672,
     'L1_attn_qw': 8.0,
     'L1_attn_kw': 8.0,
     'L1_attn_vw': 7.716,
     'L1_attn_ow': 7.742,
     'L1_ffn_router_w': 8.0,
     'L1_ffn_w1': 8.0,
     'L1_ffn_w2': 8.0}
    for name, (base, spread) in spreads.items():
        noise = np.random.default_rng([zlib.crc32(name.encode()), seed]).standard_normal(out[name].shape)
        drawn = base * np.exp(spread * noise) if base else spread * noise
        out[name] = jnp.asarray(drawn.astype(out[name].dtype))
    for name, factor in factors.items():
        out[name] = (out[name] * factor).astype(out[name].dtype)
    return out
```

```python
from contextlib import ExitStack

import numpy as np

import concourse.bass as bass
from concourse import mybir

ALU = mybir.AluOpType
ACT = mybir.ActivationFunctionType
F32 = mybir.dt.float32
F16 = mybir.dt.float16
BF16 = mybir.dt.bfloat16
I32 = mybir.dt.int32
U32 = mybir.dt.uint32
AX_X = mybir.AxisListType.X

P = 128
B, L, D = 16, 512, 128
NT = L // P
H, HD = 16, 8
G = H // 4
QR = 32
NR0, TOPK, ED = 16, 4, 64
NC = 1 + NR0 * ED // P
KVW = 2 * D + 1 + NR0
E1, F1 = 8, 512
FC = F1 // P
CAP = B * L + P
NTILE = B * NT + E1
U = 4
EPS = 1e-5
EPS_Z = 1e-4
BIG = 256.0
NSENT = 4

K_ID, K_NEG, K_BD, K_TRI, K_ONE, K_SINB, K_COSB, K_RC, K_RS, K_SEL, K_EK, K_SC, K_E, K_J = range(14)
WIDTHS = [P, P, P, P, P, L, L, L, L, 8 * P, P, 2 * NT, 3 * E1 + 1, NTILE]
KO = np.concatenate([[0], np.cumsum(WIDTHS)]).astype(int)


def constants():
    f = np.float32
    t = np.zeros((P, int(KO[-1])), f)

    def put(k, v):
        t[:, KO[k]:KO[k + 1]] = v

    i = np.arange(P)
    put(K_ID, np.eye(P))
    put(K_NEG, np.where(i[None, :] > i[:, None], -1e10, 0.0))
    put(K_BD, (i[:, None] // HD == i[None, :] // HD))
    put(K_TRI, (i[:, None] < i[None, :]))
    put(K_ONE, 1.0)
    idx = (f(np.pi / 2) * np.arange(1, L + 1, dtype=f) / f(L)).astype(f)
    put(K_SINB, np.sin(idx).astype(f)[None, :])
    put(K_COSB, np.cos(idx).astype(f)[None, :])
    sc = np.stack([np.sin(idx).reshape(NT, P).T, np.cos(idx).reshape(NT, P).T], 1).astype(f)
    put(K_SC, sc.reshape(P, 2 * NT))
    inv = (f(1.0) / np.power(f(10000.0), np.arange(0, HD, 2, dtype=f) / f(HD))).astype(f)
    ang = (np.arange(L, dtype=f)[None, :] * inv[(i % HD) // 2][:, None]).astype(f)
    put(K_RC, np.cos(ang))
    put(K_RS, np.sin(ang) * np.where(i % 2 == 0, -1.0, 1.0)[:, None])
    sel = np.zeros((P, 8, P), f)
    for c in range(8):
        for part in range(3):
            for m in range(P):
                sel[part * NR0 + 2 * c + m // ED, c, m] = 1.0
    put(K_SEL, sel.reshape(P, 8 * P))
    ek = np.zeros((P, P), f)
    ek[0::QR] = BIG
    ek[1::QR] = 1.0
    put(K_EK, ek)
    put(K_E, np.concatenate([np.arange(E1) * CAP, E1 - np.arange(E1), np.arange(E1 + 1)])[None, :].astype(f))
    put(K_J, np.arange(NTILE)[None, :])
    return t


class Flow:

    def __init__(self, nc, plan):
        self.nc, self.plan, self.seen = nc, plan, {}
        self.base, self.n, self.sems, self.events = {}, {}, {}, {}
        self.loop, self.turn, self.turns = None, None, 1

    def sem(self, name, handle, credit):
        self.sems[name], self.base[name], self.n[name] = handle, credit, 0
        if credit:
            self.nc.sync.nop().then_inc(handle, credit)

    def mark(self, ins, name, sem, by=1):
        ins.then_inc(self.sems[sem], by)
        self.n[sem] += by
        self.events[name] = (sem, self.loop, self.base[sem], self.n[sem], None)
        if self.loop:
            self.seen[(self.loop, name)] = self.n[sem]

    def value(self, name):
        if name[0] == "<":
            k = self.plan.get((self.loop, name[1:]))
            assert k is not None or not self.plan, name
            sem = self.plan.get((self.loop, name[1:], "sem"), "pe")
            step = self.plan.get((self.loop, sem), 1)
            return sem, self.base[sem] + (k or 1) - step, step
        sem, loop, base, k, step = self.events[name]
        if loop is None or step is not None:
            return sem, base + (step or 0) + k, 0
        assert loop == self.loop, name
        return sem, base + k, self.plan.get((loop, sem), 1)

    def wait(self, eng, *names):
        most = {}
        for name in filter(None, names):
            sem, const, step = self.value(name)
            if sem not in most or most[sem][0] < const:
                most[sem] = const, step
        for sem, (const, step) in most.items():
            eng.wait_ge(self.sems[sem], self.turn * step + const if step else const)

    def enter(self, loop, turn, turns):
        for s in self.n:
            self.base[s] += self.n[s]
            self.n[s] = 0
        self.events = {k: (s, lo, b, n, st) for k, (s, lo, b, n, st) in self.events.items()}
        self.loop, self.turn, self.turns = loop, turn, turns

    def leave(self):
        for name, (s, lo, b, n, st) in list(self.events.items()):
            if lo == self.loop:
                self.events[name] = (s, lo, b, n, (self.turns - 1) * self.n[s])
                self.seen[(lo, name, "sem")] = s
        for s in self.n:
            self.seen[(self.loop, s)] = self.n[s]
            self.base[s] += self.turns * self.n[s]
            self.n[s] = 0
        self.loop = None


def program(nc, io, plan):
    pe, act, dve, pool, sp = nc.tensor, nc.scalar, nc.vector, nc.gpsimd, nc.sync
    fl = Flow(nc, plan)
    ctx = ExitStack()
    with ctx:
        where = [ctx]

        def sb(name, shape, dt=F32):
            return where[-1].enter_context(nc.sbuf_tensor(name, shape, dt))

        def sem(name, credit=1024):
            fl.sem(name, ctx.enter_context(nc.semaphore("s_" + name)), credit)

        junk = ctx.enter_context(nc.semaphore("s_junk"))
        for s in ("pe", "act", "dve", "pool"):
            sem(s)
        for s in ("in", "w", "w1", "relay_out", "relay_in", "pad", "xs", "ys", "out"):
            sem(s)
        for s in ("scatter", "gather0", "gather1"):
            sem(s, 0)

        def alone(eng):
            eng.sem_inc(junk, 1)

        M, W = fl.mark, fl.wait

        X = sb("X", [P, B * NT, D])
        w1 = sb("w1", [P, E1 * 2 * F1])
        w2 = sb("w2", [P, E1 * FC * D])
        kc = sb("kc", [P, int(KO[-1])])
        wq = sb("wq", [P, D])
        wkv = sb("wkv", [P, KVW])
        bkv = sb("bkv", [P, KVW])
        wo = sb("wo", [P, D])
        up = sb("up", [P, NC * P])
        down = sb("down", [P, NC, D])
        cols = sb("cols", [P, 2])
        qk16 = sb("qk16", [P, 4 * D], F16)
        v16 = sb("v16", [P, D], F16)
        o16 = sb("o16", [P, D], F16)
        rw1 = sb("rw1", [P, E1])
        rb1 = sb("rb1", [P, E1])
        wo1 = sb("wo1", [P, D])

        def k(i):
            return kc[:, int(KO[i]):int(KO[i + 1])]

        ident = k(K_ID)
        identb = sb("identb", [P, P], BF16)
        identh = sb("identh", [P, P], F16)
        negb = sb("negb", [P, P], BF16)
        trib = sb("trib", [P, P], BF16)
        oneb = sb("oneb", [P, P], BF16)
        selb = sb("selb", [P, 8, P], BF16)
        ekh = sb("ekh", [P, P], F16)
        neghalf = sb("neghalf", [P, NT])
        zeros = sb("zeros", [P, D])

        st = sb("st", [P, NT, 6])
        mv = sb("mv", [P, NT, 2])
        ve = sb("ve", [P, NT])
        rstd = sb("rstd", [P, NT])
        xn = sb("xn", [P, NT, D])
        xnT = sb("xnT", [P, L])
        px = sb("px", [P, NT, NR0 + NSENT])
        vp = sb("vp", [P, NT, H, QR])
        mt = sb("mt", [P, 2, NT, 4, QR], F16)
        base = sb("base", [P, E1])
        slots = sb("slots", [P, B * NT])
        pmax = sb("pmax", [P, B * NT])

        PS = ctx.enter_context(nc.psum_tensor("PS", [P, 8, L], F32))

        x_d = io["x"].rearrange("b (t p) d -> p b t d", p=P)
        out_d = io["out"].rearrange("b (t p) d -> p b t d", p=P)
        relay = {n: nc.dram_tensor("relay_" + n, [H, 4, HD, L], F16, kind="Internal").ap() for n in "qk"}
        xs_d = nc.dram_tensor("xs", [(E1 + 1) * CAP, D], F32, kind="Internal").ap()
        ys_d = nc.dram_tensor("ys", [NTILE * P, D], F32, kind="Internal").ap()

        M(sp.dma_start(X[:, 0:NT, :], x_d[:, 0]), "x first", "in", 16)
        for dst, src in ((kc[:, :], io["consts"]), (wkv[:, :], io["wkv"]), (bkv[:, :], io["bkv"]),
                         (wq[:, :], io["wq"]), (wo[:, :], io["wo"]), (cols[:, :], io["cols"]),
                         (up[:, :], io["up"]), (down[:, :, :], io["down"]),
                         (qk16[:, :], io["qk16"]), (v16[:, :], io["v16"]), (o16[:, :], io["o16"]),
                         (rw1[:, :], io["rw1"]), (rb1[:, :], io["rb1"])):
            M(act.dma_start(dst, src), "weights", "w", 16)
        M(sp.dma_start(X[:, NT:, :], x_d[:, 1:].rearrange("p b t d -> p (b t) d")), "x", "in", 16)
        M(sp.dma_start(w1[:, :], io["w1"]), "w1", "w1", 16)
        M(sp.dma_start(w2[:, :], io["w2"]), "w1", "w1", 16)

        for e in (pe, act, dve, pool):
            W(e, "weights", "x")
        act.copy(identb[:, :], ident)
        act.copy(identh[:, :], ident)
        act.copy(negb[:, :], k(K_NEG))
        act.copy(trib[:, :], k(K_TRI))
        act.copy(oneb[:, :], k(K_ONE))
        act.copy(ekh[:, :], k(K_EK))
        act.copy(wo1[:, :], o16[:, :])
        M(act.copy(selb[:, :, :].rearrange("p a b -> p (a b)"), k(K_SEL)), "casts", "act")
        pool.memset(neghalf[:, :], -0.5)
        pool.memset(zeros[:, :], 0.0)
        pool.memset(mt[:, :, :, :, :], 0.0)
        pool.memset(vp[:, :, :, :], 0.0)
        M(pool.memset(px[:, :, NR0:], -1.0), "fills", "pool")
        W(pool, "fills")
        M(pool.memset(vp[:, :, :, HD:HD + 1], 1.0), "ones in v", "pool")
        M(dve.tensor_copy(base[:, :], kc[:, int(KO[K_E]):int(KO[K_E]) + E1]), "base", "dve")
        for e in (pe, act, dve, pool):
            W(e, "casts", "ones in v", "base")

        def norm(n, xt, *free):
            for t in range(NT):
                m = dve.bn_stats(st[:, t, :], xt[:, t, :])
            M(m, n + "stats", "dve")
            W(dve, n + "stats")
            alone(dve)
            for t in range(NT):
                m = dve.bn_aggr(mv[:, t, :], st[:, t, :])
            M(m, n + "mean", "dve")
            W(pool, n + "mean")
            alone(pool)
            M(pool.tensor_scalar(ve[:, :], mv[:, :, 1], EPS, None, ALU.add), n + "var", "pool")
            W(pool, n + "var")
            M(pool.tensor_tensor(rstd[:, :], ve[:, :], neghalf[:, :], ALU.pow), n + "rstd", "pool")
            W(dve, n + "rstd", *free)
            for t in range(NT):
                m = dve.tensor_scalar(xn[:, t, :], xt[:, t, :], mv[:, t, 0:1], rstd[:, t:t + 1],
                                      ALU.subtract, ALU.mult)
            M(m, n + "xn", "dve")

        def softmax(n, src, width, mx, ex, sm, rs, out):
            M(dve.tensor_reduce(mx, src, AX_X, ALU.max), n + "mx", "dve")
            W(dve, n + "mx")
            M(dve.tensor_tensor(ex, src, mx.unsqueeze(2).to_broadcast([P, NT, width]), ALU.subtract), n + "sub", "dve")
            W(act, n + "sub")
            M(act.activation(ex, ex, ACT.Exp), n + "exp", "act")
            W(dve, n + "exp")
            M(dve.tensor_reduce(sm, ex, AX_X, ALU.add), n + "sum", "dve")
            W(dve, n + "sum")
            M(dve.reciprocal(rs, sm), n + "rs", "dve")
            W(dve, n + "rs")
            M(dve.tensor_tensor(out, ex, rs.unsqueeze(2).to_broadcast([P, NT, width]), ALU.mult), n + "p", "dve")

        where.append(ctx.enter_context(ExitStack()))
        kvr = sb("kvr", [P, NT, KVW])
        ks = sb("ks", [P, NT, 2, D])
        qT = sb("qT", [P, L])
        qs = sb("qs", [P, 2, L])
        kvm = sb("kvm", [P, 2, D])
        dm = sb("dm", [P, 2, D])
        den = sb("den", [P, L])
        rden = sb("rden", [P, L])
        at0 = sb("at0", [P, L])
        mx0 = sb("mx0", [P, NT])
        sm0 = sb("sm0", [P, NT])
        rs0 = sb("rs0", [P, NT])
        e0 = sb("e0", [P, NT, NR0])
        ee0 = sb("ee0", [P, NT, NR0])
        top = sb("top", [P, NT, 8])
        rest = sb("rest", [P, NT, NR0 + NSENT])
        gate = sb("gate", [P, NT, NR0])
        gres = sb("gres", [P, NT, NR0])
        g3 = sb("g3", [P, NT, 3 * NR0], BF16)
        gT = sb("gT", [3 * NR0, L], BF16)
        hid = sb("hid", [P, 3, L])
        hg = sb("hg", [P, 3, L])
        yT = sb("yT", [P, L])

        with nc.Fori(0, B) as b:
            fl.enter("layer 0", b, B)
            xt = X[:, bass.ds(b * NT, NT), :]

            norm("", xt, "<xnT done")

            W(pe, "xn", "<y out")
            for t in range(NT):
                m = pe.transpose(PS[:, 0, t * P:(t + 1) * P], xn[:, t, :], ident)
            M(m, "xnT done", "pe")
            W(act, "xnT done", "<ups")
            M(act.copy(xnT[:, :], PS[:, 0, :]), "xnT", "act")

            W(pe, "xnT")
            for t in range(NT):
                if t >= 2:
                    W(pe, f"kvr {t - 2}")
                M(pe.matmul(PS[:, 1 + t % 2, 0:KVW], xnT[:, t * P:(t + 1) * P], wkv[:, :], start=True, stop=True),
                  f"kvr mm {t}", "pe")
                W(dve, f"kvr mm {t}")
                M(dve.tensor_tensor(kvr[:, t, :], PS[:, 1 + t % 2, 0:KVW], bkv[:, :], ALU.add), f"kvr {t}", "dve")
                W(dve, f"kvr {t}")
                for s in range(2):
                    m = dve.tensor_scalar(ks[:, t, s, :], kvr[:, t, 0:D], 0.0,
                                          k(K_SC)[:, s * NT + t:s * NT + t + 1], ALU.max, ALU.mult)
                M(m, f"k sin cos {t}", "dve")

            M(pe.matmul(PS[:, 3, :], wq[:, :], xnT[:, :], start=True, stop=True), "q mm", "pe")
            W(act, "q mm")
            M(act.activation(qT[:, :], PS[:, 3, :], ACT.Relu, bias=cols[:, 0:1]), "q", "act")
            W(pool, "q")
            pool.tensor_tensor(qs[:, 0, :], qT[:, :], k(K_SINB), ALU.mult)
            M(pool.tensor_tensor(qs[:, 1, :], qT[:, :], k(K_COSB), ALU.mult), "q sin cos", "pool")

            W(pe, f"k sin cos {NT - 1}")
            for s in range(2):
                for t in range(NT):
                    m = pe.matmul(PS[:, 1, s * 256:s * 256 + D + 1], ks[:, t, s, :], kvr[:, t, D:2 * D + 1],
                                  start=(t == 0), stop=(t == NT - 1))
            M(m, "kv mm", "pe")
            W(dve, "kv mm")
            for s in range(2):
                dve.tensor_tensor(kvm[:, s, :], PS[:, 1, s * 256:s * 256 + D], k(K_BD), ALU.mult)
                m = dve.tensor_scalar(dm[:, s, :], k(K_BD), PS[:, 1, s * 256 + D:s * 256 + D + 1], None, ALU.mult)
            M(m, "kv", "dve")
            W(pe, "kv", "q sin cos")
            for s in range(2):
                pe.matmul(PS[:, 2, :], kvm[:, s, :], qs[:, s, :], start=(s == 0), stop=(s == 1))
            for s in range(2):
                m = pe.matmul(PS[:, 3, :], dm[:, s, :], qs[:, s, :], start=(s == 0), stop=(s == 1))
            M(m, "attn mm", "pe")
            W(dve, "attn mm")
            M(dve.tensor_scalar(den[:, :], PS[:, 3, :], EPS_Z, None, ALU.max), "den", "dve")
            W(dve, "den")
            M(dve.reciprocal(rden[:, :], den[:, :]), "rden", "dve")
            W(dve, "rden")
            M(dve.tensor_tensor(at0[:, :], PS[:, 2, :], rden[:, :], ALU.mult), "attn", "dve")

            softmax("r0 ", kvr[:, :, 2 * D + 1:], NR0, mx0[:, :], e0[:, :, :], sm0[:, :], rs0[:, :], px[:, :, 0:NR0])
            W(dve, "r0 p")
            alone(dve)
            for t in range(NT):
                m = dve.max(top[:, t, :], px[:, t, 0:NR0])
            M(m, "top", "dve")
            W(dve, "top")
            M(dve.memset(top[:, :, TOPK:], -1.0), "top four", "dve")
            W(dve, "top four")
            alone(dve)
            for t in range(NT):
                m = dve.match_replace(rest[:, t, :], top[:, t, :], px[:, t, :], 0.0)
            M(m, "rest", "dve")
            W(dve, "rest")
            M(dve.tensor_tensor(gate[:, :, :], px[:, :, 0:NR0], rest[:, :, 0:NR0], ALU.subtract), "gate", "dve")
            W(dve, "gate")
            M(dve.tensor_copy(g3[:, :, 0:NR0], gate[:, :, :]), "g part 0", "dve")
            W(dve, "g part 0")
            M(dve.tensor_tensor(gres[:, :, :], gate[:, :, :], g3[:, :, 0:NR0], ALU.subtract), "g rest 0", "dve")
            W(dve, "g rest 0")
            M(dve.tensor_copy(g3[:, :, NR0:2 * NR0], gres[:, :, :]), "g part 1", "dve")
            W(dve, "g part 1")
            M(dve.tensor_tensor(g3[:, :, 2 * NR0:], gres[:, :, :], g3[:, :, NR0:2 * NR0], ALU.subtract), "g parts", "dve")
            W(pe, "g parts")
            gps = PS[:, 0, :].bitcast(BF16)
            W(pe, "xnT")
            alone(pe)
            for t in range(NT):
                m = pe.transpose(gps[0:3 * NR0, t * P:(t + 1) * P], g3[:, t, :], identb[:, :])
            M(m, "gT mm", "pe")
            W(act, "gT mm", "<downs")
            M(act.copy(gT[:, :], gps[0:3 * NR0, 0:L]), "gT", "act")

            def up_chunk(c):
                W(pe, c >= 2 and f"gelu {c - 2}")
                m = pe.matmul(PS[:, 4 + c % 2, :], up[:, c * P:(c + 1) * P], xnT[:, :], start=True, stop=True)
                M(m, "ups" if c == NC - 1 else f"up {c}", "pe")
                if c:
                    W(pe, c == 1 and "gT", "attn" if c < 3 else f"gated {c - 2}")
                    alone(pe)
                    M(pe.matmul(PS[:, 2 + c % 2, :], selb[0:3 * NR0, c - 1, :], gT[:, :], start=True, stop=True),
                      f"gate mm {c}", "pe")
                W(act, "ups" if c == NC - 1 else f"up {c}", c == 3 and "down 0", c > 3 and f"gated {c - 3}")
                M(act.activation(hid[:, c % 3, :], PS[:, 4 + c % 2, :], ACT.Gelu), f"gelu {c}", "act")
                if c:
                    W(dve, f"gelu {c}", f"gate mm {c}", c >= 4 and f"down {c - 3}")
                    M(dve.tensor_tensor(hg[:, c % 3, :], hid[:, c % 3, :], PS[:, 2 + c % 2, :], ALU.mult),
                      f"gated {c}", "dve")

            def down_chunk(c):
                W(pe, f"gated {c}" if c else "gelu 0")
                src = hg[:, c % 3, :] if c else hid[:, 0, :]
                m = pe.matmul(PS[:, 6, :], down[:, c, :], src, start=(c == 0), stop=False)
                M(m, f"down {c}", "pe")

            for c in range(NC + 2):
                if c < NC:
                    up_chunk(c)
                if c >= 2:
                    down_chunk(c - 2)
            M(pe.matmul(PS[:, 6, :], wo[:, :], at0[:, :], start=False, stop=True), "downs", "pe")
            W(act, "downs")
            M(act.activation(yT[:, :], PS[:, 6, :], ACT.Identity, bias=cols[:, 1:2]), "yT", "act")
            W(pe, "yT", "gT")
            for t in range(NT):
                m = pe.transpose(PS[:, 0, t * P:(t + 1) * P], yT[:, t * P:(t + 1) * P], ident)
            M(m, "y mm", "pe")
            W(dve, "y mm")
            M(dve.tensor_tensor(xt, xt, PS[:, 0, :].rearrange("p (t d) -> p t d", t=NT), ALU.add), "y out", "dve")
            W(dve, "y out")
            fl.leave()

        for e in (pe, act, dve, pool):
            for n in ("y out", "downs", "yT", "q sin cos"):
                W(e, n)

        where.pop().close()
        where.append(ctx.enter_context(ExitStack()))
        xh = sb("xh", [P, L], F16)
        xl = sb("xl", [P, L], F16)
        ra = sb("ra", [P, 2, L])
        rb = sb("rb", [P, 2, L])
        rq = sb("rq", [P, 2, L])
        qkh = sb("qkh", [P, 2, L], F16)
        qkl = sb("qkl", [P, 2, L], F16)
        qp = sb("qp", [P, G, L], F16)
        kp = sb("kp", [P, G, L], F16)
        nm = sb("nm", [P, 2, NT, 4])
        mrow = sb("mrow", [P, 2, L], F16)
        pt = sb("pt", [P, 3, 2, L])
        ot = sb("ot", [P, L])
        rsum = sb("rsum", [P, NT, 4])
        merged = sb("merged", [P, NT, H, HD])
        mT = sb("mT", [P, L])

        lg1 = sb("lg1", [P, NT, E1])
        s1 = sb("s1", [P, 5, NT])
        e1 = sb("e1", [P, NT, E1])
        p1 = sb("p1", [P, NT, E1])
        oh = sb("oh", [P, NT, E1])
        ohb = sb("ohb", [P, NT, E1], BF16)
        rk = sb("rk", [P, NT, E1])
        slotf = sb("slotf", [P, NT])

        with nc.Fori(0, B) as b:
            fl.enter("layer 1", b, B)
            xt = X[:, bass.ds(b * NT, NT), :]

            norm("", xt, "<xnT done", "<sorted")

            W(pe, "xn", "<x2")
            for t in range(NT):
                m = pe.transpose(PS[:, 7, t * P:(t + 1) * P], xn[:, t, :], ident)
            M(m, "xnT done", "pe")
            W(act, "xnT done", "<v mm", "<logits mm")
            M(act.copy(xnT[:, :], PS[:, 7, :]), "xnT", "act")
            M(act.copy(xh[:, :], PS[:, 7, :]), "xh", "act")
            W(dve, "xh", "<v mm")
            M(dve.tensor_tensor(xl[:, :], PS[:, 7, :], xh[:, :], ALU.subtract), "xl", "dve")

            W(pe, "xl")
            for i in range(4):
                pe.matmul(PS[:, i, :], qk16[:, i * D:(i + 1) * D], xh[:, :], start=True, stop=False)
                m = pe.matmul(PS[:, i, :], qk16[:, i * D:(i + 1) * D], xl[:, :], start=False, stop=True)
                M(m, f"qk mm {i}", "pe")
            for t in range(NT):
                pe.matmul(PS[:, 4, t * P:(t + 1) * P], xh[:, t * P:(t + 1) * P], v16[:, :], start=True, stop=False)
                m = pe.matmul(PS[:, 4, t * P:(t + 1) * P], xl[:, t * P:(t + 1) * P], v16[:, :], start=False, stop=True)
            M(m, "v mm", "pe")
            for t in range(NT):
                m = pe.matmul(PS[:, 5, t * E1:(t + 1) * E1], xnT[:, t * P:(t + 1) * P], rw1[:, :], start=True, stop=True)
            M(m, "logits mm", "pe")
            W(act, "v mm", "<pv")
            M(act.copy(vp[:, :, :, 0:HD], PS[:, 4, :].rearrange("p (t h d) -> p t h d", t=NT, h=H)), "v", "act")

            for i in range(2):
                W(dve, f"qk mm {2 * i + 1}", i == 0 and "<rotated 1")
                dve.tensor_tensor(ra[:, i, :], PS[:, 2 * i, :], k(K_RC), ALU.mult)
                M(dve.tensor_tensor(rb[:, i, :], PS[:, 2 * i + 1, :], k(K_RS), ALU.mult), f"rope {i}", "dve")
                W(pool, f"rope {i}")
                M(pool.tensor_tensor(rq[:, i, :], ra[:, i, :], rb[:, i, :], ALU.add), f"rotated {i}", "pool")
                W(act, f"rotated {i}", i == 0 and "<relayed out")
                M(act.copy(qkh[:, i, :], rq[:, i, :]), f"high {i}", "act")
                W(dve, f"high {i}")
                M(dve.tensor_tensor(qkl[:, i, :], rq[:, i, :], qkh[:, i, :], ALU.subtract), f"low {i}", "dve")
            W(sp, "low 1", "<relayed in")
            for i, (n, order) in enumerate((("q", "hlhl"), ("k", "hllh"))):
                for c, part in enumerate(order):
                    src = qkh if part == "h" else qkl
                    M(sp.dma_start(relay[n][:, c], src[:, i, :]), "relayed out", "relay_out", 16)
            W(sp, "relayed out", "<scores all")
            for n, dst in (("q", qp), ("k", kp)):
                M(sp.dma_start(dst[:, :, :], relay[n].rearrange("(g j) c d l -> g (j c d) l", g=G).rearrange("g p l -> p g l")),
                  "relayed in", "relay_in", 16)

            W(dve, "logits mm")
            M(dve.tensor_tensor(lg1[:, :, :], PS[:, 5, 0:NT * E1].rearrange("p (t e) -> p t e", t=NT),
                                rb1[:, :].unsqueeze(1).to_broadcast([P, NT, E1]), ALU.add), "logits", "dve")
            W(dve, "logits")
            softmax("r1 ", lg1[:, :, :], E1, s1[:, 0, :], e1[:, :, :], s1[:, 1, :], s1[:, 2, :], p1[:, :, :])
            W(dve, "r1 p")
            pm = pmax[:, bass.ds(b * NT, NT)]
            dve.tensor_reduce(s1[:, 3, :], p1[:, :, :], AX_X, ALU.max)
            M(dve.tensor_reduce(pm, p1[:, :, :], AX_X, ALU.max), "p max", "dve")
            W(dve, "p max")
            desc = kc[:, int(KO[K_E]) + E1:int(KO[K_E]) + 2 * E1].unsqueeze(1).to_broadcast([P, NT, E1])
            M(dve.tensor_tensor(rk[:, :, :], p1[:, :, :], s1[:, 3, :].unsqueeze(2).to_broadcast([P, NT, E1]),
                                ALU.is_equal), "is max", "dve")
            W(dve, "is max")
            M(dve.tensor_tensor(rk[:, :, :], rk[:, :, :], desc, ALU.mult), "order", "dve")
            W(dve, "order")
            M(dve.tensor_reduce(s1[:, 4, :], rk[:, :, :], AX_X, ALU.max), "first", "dve")
            W(dve, "first", "<ranks mm")
            dve.tensor_tensor(ohb[:, :, :], s1[:, 4, :].unsqueeze(2).to_broadcast([P, NT, E1]), desc, ALU.is_equal)
            M(dve.tensor_tensor(oh[:, :, :], s1[:, 4, :].unsqueeze(2).to_broadcast([P, NT, E1]), desc, ALU.is_equal),
              "one hot", "dve")
            W(pe, "one hot")
            for t in range(NT + 1):
                o = PS[:, 6, t * E1:(t + 1) * E1]
                for s in range(t):
                    m = pe.matmul(o, oneb[:, :], ohb[:, s, :], start=(s == 0), stop=(t == NT and s == NT - 1))
                if t < NT:
                    m = pe.matmul(o, trib[:, :], ohb[:, t, :], start=(t == 0), stop=True)
            M(m, "ranks mm", "pe")
            W(dve, "ranks mm")
            M(dve.tensor_tensor(rk[:, :, :], PS[:, 6, 0:NT * E1].rearrange("p (t e) -> p t e", t=NT),
                                base[:, :].unsqueeze(1).to_broadcast([P, NT, E1]), ALU.add), "rows", "dve")
            W(dve, "rows")
            dve.tensor_tensor(base[:, :], base[:, :], PS[:, 6, NT * E1:(NT + 1) * E1], ALU.add)
            M(dve.tensor_tensor(rk[:, :, :], rk[:, :, :], oh[:, :, :], ALU.mult), "row of its", "dve")
            W(dve, "row of its")
            M(dve.tensor_reduce(slotf[:, :], rk[:, :, :], AX_X, ALU.add), "slot", "dve")
            W(dve, "slot", "<sorted")
            dve.tensor_copy(slots[:, bass.ds(b * NT, NT)], slotf[:, :])
            M(dve.tensor_copy(s1[:, 3, :].bitcast(U32), slotf[:, :]), "slots", "dve")
            W(pool, "slots")
            alone(pool)
            for t in range(NT):
                M(pool.indirect_dma_start(xs_d, bass.IndirectOffsetOnAxis(ap=s1[:, 3, t:t + 1].bitcast(U32), axis=0),
                                          xn[:, t, :], None), "sorted", "scatter", 16)

            def s_unit(g, pr, qt):
                n = f"{g}.{pr}.{qt}"
                u = (g * 2 + pr) * NT + qt
                N = (qt + 1) * P
                if u == 0:
                    W(pe, "relayed in", "rope 0")
                else:
                    W(pe, f"max {u - 1}")
                alone(pe)
                for i in range(2):
                    j = (2 * pr + i) * QR
                    pe.matmul(PS[:, i, 0:N], qp[j:j + QR, g, qt * P:(qt + 1) * P], kp[j:j + QR, g, 0:N],
                              start=True, stop=False, skip_group_check=True)
                for i in range(2):
                    m = pe.matmul(PS[:, i, qt * P:N], identb[:, :], negb[:, :], start=False, stop=True,
                                  skip_group_check=True)
                M(m, f"s mm {u}", "pe")
                W(dve, f"s mm {u}")
                M(dve.tensor_reduce(nm[:, g % 2, qt, 2 * pr:2 * pr + 2], PS[:, 0:2, 0:N], AX_X, ALU.max, negate=True),
                  f"max {u}", "dve")

            def rowmax(g):
                W(dve, f"m mm {g - 2}" if g > 1 else f"<m mm {G - 2 + g}", f"max {8 * g + 7}")
                M(dve.tensor_scalar(mt[:, g % 2, :, :, 0], nm[:, g % 2, :, :], 1.0 / BIG, None, ALU.mult),
                  f"m high {g}", "dve")
                W(dve, f"m high {g}")
                M(dve.scalar_tensor_tensor(out=mt[:, g % 2, :, :, 1], in0=mt[:, g % 2, :, :, 0], scalar=-BIG,
                                           in1=nm[:, g % 2, :, :], op0=ALU.mult, op1=ALU.add), f"m low {g}", "dve")
                W(pe, f"m low {g}", f"norm {g - 2}" if g > 1 else "m row 0" if g else "xl")
                ps = PS[:, 7, :].bitcast(F16)
                for t in range(NT):
                    m = pe.transpose(ps[:, t * P:(t + 1) * P],
                                     mt[:, g % 2, t, :, :].rearrange("p a b -> p (a b)"), identh[:, :])
                M(m, f"m mm {g}", "pe")
                W(act, f"m mm {g}", "<scores all" if g < 2 else f"st mm {8 * (g - 1) - 1}")
                M(act.copy(mrow[:, g % 2, :], ps[:, 0:L]), f"m row {g}", "act")

            def st_unit(g, pr, kt):
                u = (g * 2 + pr) * NT + kt
                N = L - kt * P
                bank = 2 + 2 * (u % 2)
                W(pe, *([f"exp {u - 2}"] if u >= 2 else ["v", "logits"] if u else ["rope 1"]),
                  u % 8 == 0 and f"m row {g}")
                alone(pe)
                for i in range(2):
                    j = (2 * pr + i) * QR
                    pe.matmul(PS[:, bank + i, 0:N], kp[j:j + QR, g, kt * P:(kt + 1) * P], qp[j:j + QR, g, kt * P:],
                              start=True, stop=False, skip_group_check=True)
                for i in range(2):
                    j = (2 * pr + i) * QR
                    m = pe.matmul(PS[:, bank + i, 0:N], ekh[j:j + QR, :], mrow[j:j + QR, g % 2, kt * P:],
                                  start=False, stop=True, skip_group_check=True)
                M(m, f"st mm {u}" if u < 8 * G - 1 else "scores all", "pe")
                W(act, f"st mm {u}" if u < 8 * G - 1 else "scores all", u >= 3 and f"pv {u - 3}")
                M(act.activation(pt[:, u % 3, :, 0:N], PS[:, bank:bank + 2, 0:N], ACT.Exp, scale=1.0 / SCALE),
                  f"exp {u}", "act")
                W(pool, f"exp {u}")
                alone(pool)
                M(pool.affine_select(out=pt[:, u % 3, :, 0:P], in_=pt[:, u % 3, :, 0:P], compare_op=ALU.is_ge,
                                     fill=0.0, base=0, pattern=[[0, 2], [1, P]], channel_multiplier=-1),
                  f"causal {u}", "pool")

            def pv_unit(g, pr, kt):
                u = (g * 2 + pr) * NT + kt
                N = L - kt * P
                W(pe, f"causal {u}", u == 0 and "v", u == 0 and "rows", u % 8 == 0 and g > 0 and f"o copy {g - 1}")
                for i in range(2):
                    j = 2 * pr + i
                    m = pe.matmul(PS[j * QR:(j + 1) * QR, 6, kt * P:], vp[:, kt, 4 * g + j, :], pt[:, u % 3, i, 0:N],
                                  start=(kt == 0), stop=(kt == NT - 1), skip_group_check=True)
                M(m, f"pv {u}" if u < 8 * G - 1 else "pv", "pe")

            def heads_out(g):
                W(act, f"pv {8 * g + 7}" if g < G - 1 else "pv", g > 0 and f"o mm {g - 1}")
                M(act.copy(ot[:, :], PS[:, 6, :]), f"o copy {g}", "act")
                W(pe, f"o copy {g}", f"m row {g + 1}" if g < G - 1 else f"norm {g - 1}")
                for t in range(NT):
                    m = pe.transpose(PS[:, 7, t * P:(t + 1) * P], ot[:, t * P:(t + 1) * P], ident)
                M(m, f"o mm {g}", "pe")
                o = PS[:, 7, :].rearrange("p (t j c) -> p t j c", t=NT, j=4)
                W(dve, f"o mm {g}")
                M(dve.reciprocal(rsum[:, :, :], o[:, :, :, HD]), f"r sum {g}", "dve")
                W(dve, f"r sum {g}")
                M(dve.tensor_tensor(merged[:, :, 4 * g:4 * g + 4, :], o[:, :, :, 0:HD],
                                    rsum[:, :, :].unsqueeze(3).to_broadcast([P, NT, 4, HD]), ALU.mult),
                  f"norm {g}", "dve")

            units = [(g, pr, t) for g in range(G) for pr in range(2) for t in range(NT)]
            for u in range(8):
                s_unit(*units[u])
            rowmax(0)
            for u in range(8 * G + 1):
                if u < 8 * G:
                    st_unit(*units[u])
                if u + 8 < 8 * G:
                    s_unit(*units[u + 8])
                if u >= 1:
                    pv_unit(*units[u - 1])
                if u % 8 == 0 and u:
                    heads_out(u // 8 - 1) if u == 8 * G else None
                if u % 8 == 7 and u < 8 * G - 1:
                    rowmax(u // 8 + 1)
                if u % 8 == 0 and 0 < u < 8 * G:
                    heads_out(u // 8 - 1)

            W(pe, f"norm {G - 1}")
            for t in range(NT):
                m = pe.transpose(PS[:, 7, t * P:(t + 1) * P], merged[:, t, :, :].rearrange("p h d -> p (h d)"), ident)
            M(m, "mT mm", "pe")
            W(act, "mT mm")
            M(act.copy(mT[:, :], PS[:, 7, :]), "mT", "act")
            W(pe, "mT")
            for t in range(NT):
                m = pe.matmul(PS[:, 7, t * P:(t + 1) * P], mT[:, t * P:(t + 1) * P], wo1[:, :], start=True, stop=True)
            M(m, "out mm", "pe")
            W(dve, "out mm")
            M(dve.tensor_tensor(xt, xt, PS[:, 7, :].rearrange("p (t d) -> p t d", t=NT), ALU.add), "x2", "dve")
            W(dve, "x2")
            fl.leave()

        for e in (pe, act, dve, pool, sp):
            for n in ("x2", "sorted", "mT"):
                W(e, n)

        where.pop().close()
        where.append(ctx.enter_context(ExitStack()))
        ti = sb("ti", [P, 4, E1 + 1], I32)
        tf = sb("tf", [P, 6, E1 + 1])
        yrow = sb("yrow", [P, B * NT])
        ystep = sb("ystep", [P, B * NT])
        ja = sb("ja", [P, E1 + 1, NTILE])
        jb = sb("jb", [P, E1 + 1, NTILE])
        jr = sb("jr", [P, 4, NTILE])
        ji = sb("ji", [P, 3, NTILE], I32)
        xsb = sb("xsb", [P, U, D])
        xsT = sb("xsT", [P, U, P])
        sil = sb("sil", [P, 2, F1])
        act1 = sb("act1", [P, 2, F1])
        aT = sb("aT", [P, 2, F1])
        ysb = sb("ysb", [P, U, D])

        E = kc[:, int(KO[K_E]):int(KO[K_E]) + E1]
        idx9 = kc[:, int(KO[K_E]) + 2 * E1:int(KO[K_E + 1])]
        step = [0]

        def D_(ins):
            step[0] += 1
            M(ins, f"chain {step[0]}", "dve")
            W(dve, f"chain {step[0]}")

        D_(dve.tensor_copy(ti[:, 0, 0:E1], base[:, :]))
        D_(dve.tensor_tensor(tf[:, 0, 0:E1], base[:, :], E, ALU.subtract))
        D_(dve.tensor_scalar(tf[:, 0, 0:E1], tf[:, 0, 0:E1], float(P - 1), None, ALU.add))
        D_(dve.tensor_copy(ti[:, 1, 0:E1], tf[:, 0, 0:E1]))
        D_(dve.tensor_scalar(ti[:, 2, 0:E1], ti[:, 1, 0:E1], 7, None, ALU.arith_shift_right))
        D_(dve.tensor_copy(tf[:, 1, 0:E1], ti[:, 2, 0:E1]))
        D_(dve.memset(tf[:, 2, 0:1], 0.0))
        for e in range(E1):
            D_(dve.tensor_tensor(tf[:, 2, e + 1:e + 2], tf[:, 2, e:e + 1], tf[:, 1, e:e + 1], ALU.add))
        D_(dve.memset(tf[:, 3, :], 1e9))
        D_(dve.tensor_copy(tf[:, 3, 0:E1], tf[:, 2, 1:E1 + 1]))
        jj = k(K_J).unsqueeze(1).to_broadcast([P, E1 + 1, NTILE])

        def over_j(v):
            return v.unsqueeze(2).to_broadcast([P, E1 + 1, NTILE])

        D_(dve.tensor_tensor(ja[:, :, :], jj, over_j(tf[:, 2, :]), ALU.is_ge))
        D_(dve.tensor_tensor(jb[:, :, :], jj, over_j(tf[:, 3, :]), ALU.is_lt))
        D_(dve.tensor_tensor(ja[:, :, :], ja[:, :, :], jb[:, :, :], ALU.mult))
        by_j = ja[:, :, :].rearrange("p e j -> p j e")
        D_(dve.tensor_tensor(jb[:, :, :], ja[:, :, :], over_j(idx9), ALU.mult))
        D_(dve.tensor_reduce(jr[:, 0, :], jb[:, :, :].rearrange("p e j -> p j e"), AX_X, ALU.add))
        D_(dve.tensor_tensor(jb[:, :, :], ja[:, :, :], over_j(tf[:, 2, :]), ALU.mult))
        D_(dve.tensor_reduce(jr[:, 1, :], jb[:, :, :].rearrange("p e j -> p j e"), AX_X, ALU.add))
        D_(dve.tensor_tensor(jr[:, 1, :], k(K_J), jr[:, 1, :], ALU.subtract))
        D_(dve.tensor_scalar(jr[:, 1, :], jr[:, 1, :], float(P), None, ALU.mult))
        D_(dve.scalar_tensor_tensor(out=jr[:, 2, :], in0=jr[:, 0, :], scalar=float(CAP), in1=jr[:, 1, :],
                                    op0=ALU.mult, op1=ALU.add))
        D_(dve.tensor_scalar(jr[:, 3, :], jr[:, 2, :], float(E1 * CAP), None, ALU.min))
        D_(dve.tensor_scalar(jr[:, 0, :], jr[:, 0, :], float(E1 - 1), float(2 * F1), ALU.min, ALU.mult))
        D_(dve.tensor_copy(ji[:, 0, :], jr[:, 0, :]))
        D_(dve.tensor_copy(ji[:, 1, :], jr[:, 2, :]))
        D_(dve.tensor_copy(ji[:, 2, :], jr[:, 3, :]))
        D_(dve.tensor_scalar(tf[:, 4, 0:E1], tf[:, 2, 0:E1], float(P), None, ALU.mult))
        D_(dve.tensor_tensor(tf[:, 4, 0:E1], tf[:, 4, 0:E1], E, ALU.subtract))
        D_(dve.tensor_copy(yrow[:, :], slots[:, :]))
        for e in range(1, E1):
            D_(dve.tensor_tensor(tf[:, 5, 0:1], tf[:, 4, e:e + 1], tf[:, 4, e - 1:e], ALU.subtract))
            D_(dve.tensor_scalar(ystep[:, :], slots[:, :], float(e * CAP), tf[:, 5, 0:1], ALU.is_ge, ALU.mult))
            D_(dve.tensor_tensor(yrow[:, :], yrow[:, :], ystep[:, :], ALU.add))
        W(sp, f"chain {step[0]}")
        for e in range(E1):
            row = sp.value_load(ti[0:1, 0, e:e + 1], min_val=0, max_val=E1 * CAP - P)
            M(sp.dma_start(xs_d[bass.ds(row, P), :], zeros[:, :]), "pad", "pad", 16)
        M(sp.dma_start(xs_d[E1 * CAP:E1 * CAP + P, :], zeros[:, :]), "pad", "pad", 16)
        W(sp, "pad")
        W(pe, f"chain {step[0]}")
        W(act, f"chain {step[0]}")
        W(pe, "w1")

        with nc.Fori(0, NTILE // U) as it:
            fl.enter("experts", it, NTILE // U)
            W(sp, "<xsT mm")
            for u in range(U):
                row = sp.value_load(ji[0:1, 2, bass.ds(it * U + u, 1)], min_val=0, max_val=E1 * CAP)
                M(sp.dma_start(xsb[:, u, :], xs_d[bass.ds(row, P), :]), "xs in", "xs", 16)
            W(pe, "xs in", f"<y copy {U - 1}")
            for u in range(U):
                m = pe.transpose(PS[:, 0, u * P:(u + 1) * P], xsb[:, u, :], ident)
            M(m, "xsT mm", "pe")
            W(act, "xsT mm", f"<h mm {U - 1}")
            M(act.copy(xsT[:, :, :].rearrange("p u c -> p (u c)"), PS[:, 0, :]), "xsT", "act")
            W(pe, "xsT")
            offs = []

            def hidden(u):
                e1k = pe.value_load(ji[0:1, 0, bass.ds(it * U + u, 1)], min_val=0, max_val=(E1 - 1) * 2 * F1)
                offs.append(e1k)
                bk = 1 + 2 * (u % 2)
                if u >= 2:
                    W(pe, f"glu {u - 2}")
                for i in range(2):
                    m = pe.matmul(PS[:, bk + i, :], xsT[:, u, :], w1[:, bass.ds(e1k + i * F1, F1)], start=True, stop=True)
                M(m, f"h mm {u}", "pe")
                W(act, f"h mm {u}", f"glu {u - 2}" if u >= 2 else f"<glu {u + 2}")
                M(act.activation(sil[:, u % 2, :], PS[:, bk, :], ACT.Silu), f"silu {u}", "act")
                W(dve, f"silu {u}", f"aT mm {u - 2}" if u >= 2 else f"<aT mm {u + 2}")
                M(dve.tensor_tensor(act1[:, u % 2, :], sil[:, u % 2, :], PS[:, bk + 1, :], ALU.mult), f"glu {u}", "dve")

            def turned(u):
                W(pe, f"glu {u}", u > 0 and f"aT {u - 1}")
                for c in range(FC):
                    m = pe.transpose(PS[:, 5, c * P:(c + 1) * P], act1[:, u % 2, c * P:(c + 1) * P], ident)
                M(m, f"aT mm {u}", "pe")
                W(dve, f"aT mm {u}", f"y mm {u - 2}" if u >= 2 else f"<y mm {u + 2}")
                M(dve.tensor_copy(aT[:, u % 2, :], PS[:, 5, :]), f"aT {u}", "dve")

            def outputs(u):
                W(pe, f"aT {u}", u >= 2 and f"y copy {u - 2}")
                w2off = offs[u] // 2
                for c in range(FC):
                    m = pe.matmul(PS[:, 6 + u % 2, 0:D], aT[:, u % 2, c * P:(c + 1) * P],
                                  w2[:, bass.ds(w2off + c * D, D)], start=(c == 0), stop=(c == FC - 1))
                M(m, f"y mm {u}", "pe")
                W(act, f"y mm {u}", u == 0 and "<ys out")
                M(act.copy(ysb[:, u, :], PS[:, 6 + u % 2, 0:D]), f"y copy {u}", "act")
                W(sp, f"y copy {u}")
                M(sp.dma_start(ys_d[bass.ds((it * U + u) * P, P), :], ysb[:, u, :]), "ys out", "ys", 16)

            for u in range(U + 2):
                if u < U:
                    hidden(u)
                if 1 <= u <= U:
                    turned(u - 1)
                if u >= 2:
                    outputs(u - 2)
            fl.leave()

        W(pool, "ys out")
        yg = sb("yg", [P, 2, NT, D])
        with nc.Fori(0, B // 2) as it:
            fl.enter("gather", it, B // 2)
            for i in range(2):
                W(pool, f"<final {i}")
                sl = sb(f"sl{i}", [P, NT], U32)
                M(pool.tensor_copy(sl[:, :], yrow[:, bass.ds(it * 2 * NT + i * NT, NT)]), f"slots {i}", "pool")
                W(pool, f"slots {i}")
                alone(pool)
                for t in range(NT):
                    M(pool.indirect_dma_start(yg[:, i, t, :], None, ys_d,
                                              bass.IndirectOffsetOnAxis(ap=sl[:, t:t + 1], axis=0)),
                      f"gathered {i}", f"gather{i}", 16)
                W(dve, f"gathered {i}")
                for t in range(NT):
                    c = it * 2 * NT + (i * NT + t)
                    xt1 = X[:, bass.ds(c, 1), :].rearrange("p a d -> p (a d)")
                    m = dve.scalar_tensor_tensor(out=xt1, in0=yg[:, i, t, :], scalar=pmax[:, bass.ds(c, 1)],
                                                 in1=xt1, op0=ALU.mult, op1=ALU.add)
                M(m, f"final {i}", "dve")
                W(sp, f"final {i}")
                M(sp.dma_start(out_d[:, bass.ds(it * 2 + i, 1)].rearrange("p b t d -> p (b t) d"),
                               X[:, bass.ds(it * 2 * NT + i * NT, NT), :]), "out", "out", 16)
            fl.leave()
        W(sp, "out")
    for name, (s, lo, *_ ) in fl.events.items():
        if lo:
            fl.seen[(lo, name, "sem")] = s
    return fl.seen


SCALE = float(np.sqrt(np.float16(D)))

_INS = [("x", (B, L, D), "float32"), ("consts", (P, int(KO[-1])), "float32"), ("wkv", (P, KVW), "float32"),
        ("bkv", (P, KVW), "float32"), ("wq", (P, D), "float32"), ("wo", (P, D), "float32"),
        ("cols", (P, 2), "float32"), ("up", (P, NC * P), "float32"), ("down", (P, NC, D), "float32"),
        ("qk16", (P, 4 * D), "float16"), ("v16", (P, D), "float16"), ("o16", (P, D), "float16"),
        ("rw1", (P, E1), "float32"), ("rb1", (P, E1), "float32"),
        ("w1", (P, E1 * 2 * F1), "float32"), ("w2", (P, E1 * FC * D), "float32")]


def build(nc, plan):
    io = {n: nc.dram_tensor("in_" + n, list(s), mybir.dt.from_np(np.dtype(d)), kind="ExternalInput").ap()
          for n, s, d in _INS}
    io["out"] = nc.dram_tensor("out_y", [B, L, D], F32, kind="ExternalOutput").ap()
    return program(nc, io, plan)


def layouts(a):
    f = np.float32
    swap = np.arange(D) ^ 1
    t = lambda w: np.ascontiguousarray(w.T)
    up = np.concatenate([a["L0_ffn_shared_up"].reshape(-1, D), a["L0_ffn_routed_up"].reshape(-1, D)])
    dn = np.concatenate([a["L0_ffn_shared_down"], a["L0_ffn_routed_down"]])
    dn = dn.transpose(0, 2, 1).reshape(NC, P, D).transpose(1, 0, 2)
    rows = lambda v: np.broadcast_to(v[None, :], (P, v.size))
    return {
        "x": a["L0_attn_x"], "consts": constants(),
        "wkv": np.concatenate([a["L0_attn_Wk"].T, a["L0_attn_Wv"].T, np.zeros((D, 1), f), a["L0_ffn_router_w"].T], 1),
        "bkv": rows(np.concatenate([a["L0_attn_bk"], a["L0_attn_bv"], np.ones(1, f), np.zeros(NR0, f)])),
        "wq": t(a["L0_attn_Wq"]), "wo": t(a["L0_attn_Wo"]),
        "cols": np.stack([a["L0_attn_bq"], a["L0_attn_bo"]], 1), "up": t(up), "down": dn,
        "qk16": np.concatenate([a["L1_attn_qw"], a["L1_attn_qw"][:, swap], a["L1_attn_kw"], a["L1_attn_kw"][:, swap]], 1),
        "v16": a["L1_attn_vw"], "o16": a["L1_attn_ow"], "rw1": a["L1_ffn_router_w"], "rb1": rows(a["L1_ffn_router_b"]),
        "w1": a["L1_ffn_w1"].transpose(1, 0, 2).reshape(P, -1),
        "w2": a["L1_ffn_w2"].reshape(E1, FC, P, D).transpose(2, 0, 1, 3).reshape(P, -1),
    }


def kernel(**inputs):
    import concourse.bacc as _bacc
    from concourse.bass_utils import run_bass_kernel_spmd as _run

    plan = build(_bacc.Bacc("TRN2", target_bir_lowering=False, num_devices=1), {})
    nc = _bacc.Bacc("TRN2", target_bir_lowering=False, num_devices=1)
    assert build(nc, plan) == plan
    arrays = {"in_" + n: np.ascontiguousarray(v) for n, v in layouts({n: np.asarray(v) for n, v in inputs.items()}).items()}
    r = _run(nc, [arrays], core_ids=[0])
    return r.results[0]["out_y"]
```

```python
from contextlib import ExitStack

import numpy as np

import concourse.bass as bass
from concourse import mybir

ALU = mybir.AluOpType
ACT = mybir.ActivationFunctionType
F32 = mybir.dt.float32
F16 = mybir.dt.float16
BF16 = mybir.dt.bfloat16
I32 = mybir.dt.int32
U32 = mybir.dt.uint32
AX_X = mybir.AxisListType.X

P = 128
B, L, D = 16, 512, 128
NT = L // P
H, HD = 16, 8
G = H // 4
MROW = 4 * HD
NR0, TOPK, ED = 16, 4, 64
NC = 1 + NR0 * ED // P
KVW = 2 * D + 1 + NR0
E1, F1 = 8, 512
FC = F1 // P
CAP = B * L + P
NTILE = B * NT + E1
U = 4
LAG, AHEAD = 2, 4
NTAB = LAG + NTILE + AHEAD
EPS = 1e-5
EPS_Z = 1e-4
BIG = 256.0
NSENT = 4

K_ID, K_NEG, K_BD, K_TRI, K_ONE, K_SINB, K_COSB, K_RC, K_RS, K_W, K_SC, K_E, K_J = range(13)
WIDTHS = [P, P, P, P, P, L, L, L, L, 1, 2 * NT, 3 * E1 + 1, NTAB]
KO = np.concatenate([[0], np.cumsum(WIDTHS)]).astype(int)


def constants():
    f = np.float32
    t = np.zeros((P, int(KO[-1])), f)

    def put(k, v):
        t[:, KO[k]:KO[k + 1]] = v

    i = np.arange(P)
    put(K_ID, np.eye(P))
    put(K_NEG, np.where(i[None, :] > i[:, None], -1e10, 0.0))
    put(K_BD, (i[:, None] // HD == i[None, :] // HD))
    put(K_TRI, (i[:, None] < i[None, :]))
    put(K_ONE, 1.0)
    idx = (f(np.pi / 2) * np.arange(1, L + 1, dtype=f) / f(L)).astype(f)
    put(K_SINB, np.sin(idx).astype(f)[None, :])
    put(K_COSB, np.cos(idx).astype(f)[None, :])
    sc = np.stack([np.sin(idx).reshape(NT, P).T, np.cos(idx).reshape(NT, P).T], 1).astype(f)
    put(K_SC, sc.reshape(P, 2 * NT))
    inv = (f(1.0) / np.power(f(10000.0), np.arange(0, HD, 2, dtype=f) / f(HD))).astype(f)
    ang = (np.arange(L, dtype=f)[None, :] * inv[(i % HD) // 2][:, None]).astype(f)
    put(K_RC, np.cos(ang))
    put(K_RS, np.sin(ang) * np.where(i % 2 == 0, -1.0, 1.0)[:, None])
    put(K_W, np.where(i == MROW, BIG, np.where(i == MROW + 1, 1.0, 0.0))[:, None])
    put(K_E, np.concatenate([np.arange(E1) * CAP, E1 - np.arange(E1), np.arange(E1 + 1)])[None, :].astype(f))
    put(K_J, (np.arange(NTAB) - LAG)[None, :])
    return t


class Flow:

    def __init__(self, nc, plan):
        self.nc, self.plan, self.seen = nc, plan, {}
        self.base, self.n, self.sems, self.events = {}, {}, {}, {}
        self.loop, self.turn, self.turns = None, None, 1

    def sem(self, name, handle, credit):
        self.sems[name], self.base[name], self.n[name] = handle, credit, 0
        if credit:
            self.nc.sync.nop().then_inc(handle, credit)

    def mark(self, ins, name, sem, by=1):
        ins.then_inc(self.sems[sem], by)
        self.n[sem] += by
        self.events[name] = (sem, self.loop, self.base[sem] + self.n[sem])
        if self.loop:
            self.seen[(self.loop, name)] = (sem, self.n[sem])

    def value(self, name):
        maybe, name = name.startswith("?"), name.lstrip("?")
        if self.loop:
            if name in self.events and self.events[name][1] == self.loop:
                return (*self.events[name][::2], True)
            if (self.loop, name) in self.plan:
                sem, k = self.plan[(self.loop, name)]
                return sem, self.base[sem] - self.plan[(self.loop, "total", sem)] + k, True
        if name not in self.events:
            assert not self.plan or maybe, name
            return None, 0, False
        return (*self.events[name][::2], False)

    def wait(self, eng, *names):
        most = {}
        for name in filter(None, names):
            sem, const, turns = self.value(name)
            if sem and (sem not in most or most[sem] < (turns, const)):
                most[sem] = turns, const
        for i, (sem, (turns, const)) in enumerate(most.items()):
            if i and eng is self.nc.sync:
                eng.sem_inc(self.junk, 1)
            step = self.plan.get((self.loop, "total", sem), 1)
            eng.wait_ge(self.sems[sem], self.turn * step + const if turns else const)

    def all(self, eng, *sems):
        for s in sems:
            eng.wait_ge(self.sems[s], self.base[s] + self.n[s])

    def enter(self, loop, turn, turns):
        for s in self.n:
            self.base[s] += self.n[s]
            self.n[s] = 0
        self.loop, self.turn, self.turns = loop, turn, turns

    def leave(self):
        for s in self.n:
            self.seen[(self.loop, "total", s)] = self.n[s]
            rest = (self.turns - 1) * self.n[s]
            self.events = {k: (es, None, v + rest) if es == s and lo == self.loop else (es, lo, v)
                           for k, (es, lo, v) in self.events.items()}
            self.base[s] += self.turns * self.n[s]
            self.n[s] = 0
        self.loop = None


def program(nc, io, plan):
    pe, act, dve, pool, sp = nc.tensor, nc.scalar, nc.vector, nc.gpsimd, nc.sync
    fl = Flow(nc, plan)
    ctx = ExitStack()
    with ctx:
        where = [ctx]

        def sb(name, shape, dt=F32):
            return where[-1].enter_context(nc.sbuf_tensor(name, shape, dt))

        def sem(name, credit=1024):
            fl.sem(name, ctx.enter_context(nc.semaphore("s_" + name)), credit)

        junk = ctx.enter_context(nc.semaphore("s_junk"))
        fl.junk = junk
        for s in ("pe", "act", "dve", "pool"):
            sem(s)
        for s in ("in", "rest in", "w", "w1", "gate out", "gate in", "relay out", "relay in", "m0", "m1", "pad",
                  *(f"xs{u}" for u in range(U)), *(f"ys{u}" for u in range(U)), "out"):
            sem(s)
        for s in ("scatter", "gather0", "gather1"):
            sem(s, 0)

        def alone(eng):
            eng.sem_inc(junk, 1)

        M, W = fl.mark, fl.wait

        X = sb("X", [P, B * NT, D])
        kc = sb("kc", [P, int(KO[-1])])
        base = sb("base", [P, E1])
        slots = sb("slots", [P, B * NT])
        pmax = sb("pmax", [P, B * NT])
        zeros = sb("zeros", [P, D])

        def k(i):
            return kc[:, int(KO[i]):int(KO[i + 1])]

        ident = k(K_ID)
        even = sb("even", [P, 2, H, L], F16)
        w1 = even[:, :, :, :].rearrange("p s h l -> p (s h l)").bitcast(F32)
        share = sb("share", [P, (NC - 1) * L])
        w2 = share
        where.append(ctx.enter_context(ExitStack()))
        wq = sb("wq", [P, D])
        wkv = sb("wkv", [P, KVW])
        bkv = sb("bkv", [P, KVW])
        wo = sb("wo", [P, D])
        up = sb("up", [P, NC * P])
        down = sb("down", [P, NC, D])
        cols = sb("cols", [P, 2])
        qk16 = sb("qk16", [P, 4 * D], F16)
        v16 = sb("v16", [P, D], F16)
        o16 = sb("o16", [P, D], F16)
        wo1 = sb("wo1", [P, D])
        rw1 = sb("rw1", [P, E1])
        rb1 = sb("rb1", [P, E1])
        identb = sb("identb", [P, P], BF16)
        identh = sb("identh", [P, P], F16)
        negb = sb("negb", [P, P], BF16)
        trib = sb("trib", [P, P], BF16)
        oneb = sb("oneb", [P, P], BF16)
        neghalf = sb("neghalf", [P, NT])

        st = sb("st", [P, NT, 6])
        mv = sb("mv", [P, NT, 2])
        ve = sb("ve", [P, NT])
        rstd = sb("rstd", [P, NT])
        xn = sb("xn", [P, NT, D])
        xnT = sb("xnT", [P, L])
        kvr = share[:, 0:NT * KVW].rearrange("p (t c) -> p t c", t=NT)
        ks = share[:, NT * KVW:NT * KVW + 2 * L].rearrange("p (t s d) -> p t s d", t=NT, s=2)
        qs = share[:, NT * KVW + 2 * L:NT * KVW + 4 * L].rearrange("p (s l) -> p s l", s=2)
        gates = share[:, :].rearrange("p (c l) -> p c l", c=NC - 1)
        qT = sb("qT", [P, L])
        kvm = sb("kvm", [P, 2, D])
        dm = sb("dm", [P, 2, D])
        den = sb("den", [P, L])
        at0 = sb("at0", [P, L])
        sm = sb("sm", [P, 3, NT])
        e0 = sb("e0", [P, NT, NR0])
        px = sb("px", [P, NT, NR0 + NSENT])
        top = sb("top", [P, NT, 8])
        rest = sb("rest", [P, NT, NR0 + NSENT])
        gate = sb("gate", [P, NT, NR0])
        hid = sb("hid", [P, NC, L])
        yT = sb("yT", [P, L])
        gT = yT[0:NR0, :]
        xh = sb("xh", [P, L], F16)
        xl = sb("xl", [P, L], F16)
        ra = sb("ra", [P, L])
        rb = sb("rb", [P, L])
        qkh = sb("qkh", [P, 2, L], F16)
        qkl = sb("qkl", [P, 2, L], F16)
        lg1 = sb("lg1", [P, NT, E1])
        s1 = sb("s1", [P, 5, NT])
        e1 = sb("e1", [P, NT, E1])
        p1 = sb("p1", [P, NT, E1])
        oh = sb("oh", [P, NT, E1])
        ohb = sb("ohb", [P, NT, E1], BF16)
        rk = sb("rk", [P, NT, E1])
        slotu = sb("slotu", [P, NT], U32)

        qp = [even[:, 0], sb("qp1", [P, H, L], F16)]
        kp = [even[:, 1], sb("kp1", [P, H, L], F16)]
        vp = [sb(f"vp{i}", [P, NT, H, 2 * HD + 1], F16) for i in range(2)]
        nm = sb("nm", [P, 2, NT, 4])
        mt = sb("mt", [P, 2, NT, 4, 2], F16)
        mrow = sb("mrow", [8, 2, L], F16)
        pt = sb("pt", [P, 2, L])
        ph = sb("ph", [P, 4, L], F16)
        pl = sb("pl", [P, 4, L], F16)
        rsum = sb("rsum", [P, NT, 4])
        mlow = sb("mlow", [P, NT, 4, HD])
        merged = sb("merged", [P, NT, H, HD])
        mT = sb("mT", [P, L])

        PS = ctx.enter_context(nc.psum_tensor("PS", [P, 8, L], F32))
        S0, ST0, PV0, WK0 = 0, 2, 4, 6

        x_d = io["x"].rearrange("b (t p) d -> p b t d", p=P)
        out_d = io["out"].rearrange("b (t p) d -> p b t d", p=P)
        relay = {n: nc.dram_tensor("relay_" + n, [H, 4, HD, L], F16, kind="Internal").ap() for n in "qk"}
        gate_d = nc.dram_tensor("gate_rows", [NR0, L], F32, kind="Internal").ap()
        xs_d = nc.dram_tensor("xs", [(E1 + 1) * CAP, D], F32, kind="Internal").ap()
        ys_d = nc.dram_tensor("ys", [(LAG + NTILE) * P, D], F32, kind="Internal").ap()

        M(sp.dma_start(X[:, 0:NT, :], x_d[:, 0]), "x", "in", 16)
        for i, (dst, src) in enumerate((
                (kc[:, :], io["consts"]), (wkv[:, :], io["wkv"]), (bkv[:, :], io["bkv"]), (wq[:, :], io["wq"]),
                (wo[:, :], io["wo"]), (cols[:, :], io["cols"]), (up[:, :], io["up"]), (down[:, :, :], io["down"]),
                (qk16[:, :], io["qk16"]), (v16[:, :], io["v16"]), (o16[:, :], io["o16"]), (rw1[:, :], io["rw1"]),
                (rb1[:, :], io["rb1"]))):
            M((act if i % 2 else sp).dma_start(dst, src), "weights", "w", 16)
        for e in (pe, act, dve, pool):
            W(e, "weights", "x")
        M(sp.dma_start(X[:, NT:, :], x_d[:, 1:].rearrange("p b t d -> p (b t) d")), "all x", "rest in", 16)

        act.copy(identb[:, :], ident)
        act.copy(identh[:, :], ident)
        act.copy(negb[:, :], k(K_NEG))
        act.copy(trib[:, :], k(K_TRI))
        act.copy(oneb[:, :], k(K_ONE))
        M(act.copy(wo1[:, :], o16[:, :]), "casts", "act")
        pool.memset(neghalf[:, :], -0.5)
        pool.memset(zeros[:, :], 0.0)
        pool.memset(px[:, :, NR0:], -1.0)
        M(pool.memset(vp[0][:, :, :, HD:HD + 1], 1.0), "fills", "pool")
        M(pool.memset(vp[1][:, :, :, HD:HD + 1], 1.0), "fills", "pool")
        M(dve.tensor_copy(base[:, :], kc[:, int(KO[K_E]):int(KO[K_E]) + E1]), "base", "dve")
        for i in range(2):
            for n, tile in (("q", qp[i]), ("k", kp[i])):
                M(dve.memset(tile[:, :, :].rearrange("p h l -> p (h l)").bitcast(F32), 0.0), f"{n} zero {i}", "dve")
            W(act, f"k zero {i}")
            M(act.copy(kp[i][MROW:MROW + 2, :, :].rearrange("p h l -> p (h l)"),
                       kc[MROW:MROW + 2, int(KO[K_W]):int(KO[K_W]) + 1].to_broadcast([2, H * L])), "k ones", "act")
        for e in (pe, act, dve, pool, sp):
            W(e, "casts", "fills", "base", "k ones", "q zero 1")

        ring = [0, "?none", "?none", None]

        def bank(hold=False):
            i = 1 - ring[3] if ring[3] is not None else ring[0]
            ring[0] = 1 - i
            if hold:
                ring[3] = i
            return i, ring[1 + i], PS[:, WK0 + i, :]

        def norm(n, xt, *free):
            alone(dve)
            for t in range(NT):
                m = dve.bn_stats(st[:, t, :], xt[:, t, :])
            M(m, n + "stats", "dve")
            W(dve, n + "stats")
            alone(dve)
            for t in range(NT):
                m = dve.bn_aggr(mv[:, t, :], st[:, t, :])
            M(m, n + "mean", "dve")
            W(pool, n + "mean")
            alone(pool)
            M(pool.tensor_scalar(ve[:, :], mv[:, :, 1], EPS, None, ALU.add), n + "var", "pool")
            W(pool, n + "var")
            M(pool.tensor_tensor(rstd[:, :], ve[:, :], neghalf[:, :], ALU.pow), n + "rstd", "pool")
            yield
            W(dve, n + "rstd", *free)
            for t in range(NT):
                m = dve.tensor_scalar(xn[:, t, :], xt[:, t, :], mv[:, t, 0:1], rstd[:, t:t + 1],
                                      ALU.subtract, ALU.mult)
            M(m, n + "xn", "dve")
            yield

        def softmax(n, src, width, ex, out):
            M(dve.tensor_reduce(sm[:, 0, :], src, AX_X, ALU.max), n + "mx", "dve")
            W(dve, n + "mx")
            M(dve.tensor_tensor(ex, src, sm[:, 0, :].unsqueeze(2).to_broadcast([P, NT, width]), ALU.subtract),
              n + "sub", "dve")
            W(act, n + "sub")
            M(act.activation(ex, ex, ACT.Exp), n + "exp", "act")
            yield
            W(dve, n + "exp")
            M(dve.tensor_reduce(sm[:, 1, :], ex, AX_X, ALU.add), n + "sum", "dve")
            W(dve, n + "sum")
            M(dve.reciprocal(sm[:, 2, :], sm[:, 1, :]), n + "rs", "dve")
            W(dve, n + "rs")
            M(dve.tensor_tensor(out, ex, sm[:, 2, :].unsqueeze(2).to_broadcast([P, NT, width]), ALU.mult),
              n + "p", "dve")
            W(dve, n + "p")

        def turn(n, src, free):
            i, used, ps = bank()
            W(pe, free, used)
            for t in range(NT):
                m = pe.transpose(ps[:, t * P:(t + 1) * P], src(t), ident)
            M(m, n, "pe")
            return i, ps

        def first_part(b):
            xt = X[:, bass.ds(b * NT, NT), :]
            yield from norm("0 ", xt, "?0 xnT mm", "?1 xnT mm", "?sorted")

            i, ps = turn("0 xnT mm", lambda t: xn[:, t, :], "0 xn")
            W(act, "0 xnT mm", "?logits mm")
            M(act.copy(xnT[:, :], ps), "0 xnT", "act")
            ring[1 + i] = "0 xnT"
            yield

            for t in range(NT):
                i, used, ps = bank()
                W(pe, "0 xnT", used)
                M(pe.matmul(ps[:, 0:KVW], xnT[:, t * P:(t + 1) * P], wkv[:, :], start=True, stop=True),
                  f"kvr mm {t}", "pe")
                W(dve, f"kvr mm {t}", "?gated all")
                M(dve.tensor_tensor(kvr[:, t, :], ps[:, 0:KVW], bkv[:, :], ALU.add), f"kvr {t}", "dve")
                ring[1 + i] = f"kvr {t}"
                W(dve, f"kvr {t}")
                for s in range(2):
                    m = dve.tensor_scalar(ks[:, t, s, :], kvr[:, t, 0:D], 0.0,
                                          k(K_SC)[:, s * NT + t:s * NT + t + 1], ALU.max, ALU.mult)
                M(m, f"k sin cos {t}", "dve")
                yield

            i, used, ps = bank()
            W(pe, used)
            M(pe.matmul(ps, wq[:, :], xnT[:, :], start=True, stop=True), "q mm", "pe")
            W(act, "q mm", "?q sin cos")
            M(act.activation(qT[:, :], ps, ACT.Relu, bias=cols[:, 0:1]), "q", "act")
            ring[1 + i] = "q"
            W(pool, "q")
            pool.tensor_tensor(qs[:, 0, :], qT[:, :], k(K_SINB), ALU.mult)
            M(pool.tensor_tensor(qs[:, 1, :], qT[:, :], k(K_COSB), ALU.mult), "q sin cos", "pool")
            yield

            i, used, ps = bank()
            W(pe, f"k sin cos {NT - 1}", used)
            for s in range(2):
                for t in range(NT):
                    m = pe.matmul(ps[:, s * 256:s * 256 + D + 1], ks[:, t, s, :], kvr[:, t, D:2 * D + 1],
                                  start=(t == 0), stop=(t == NT - 1))
            M(m, "kv mm", "pe")
            W(dve, "kv mm", "?attn mm")
            for s in range(2):
                dve.tensor_tensor(kvm[:, s, :], ps[:, s * 256:s * 256 + D], k(K_BD), ALU.mult)
                m = dve.tensor_scalar(dm[:, s, :], k(K_BD), ps[:, s * 256 + D:s * 256 + D + 1], None, ALU.mult)
            M(m, "kv", "dve")
            ring[1 + i] = "kv"
            yield
            yield from softmax("r0 ", kvr[:, :, 2 * D + 1:], NR0, e0[:, :, :], px[:, :, 0:NR0])
            alone(dve)
            for t in range(NT):
                m = dve.max(top[:, t, :], px[:, t, 0:NR0])
            M(m, "top", "dve")
            W(dve, "top")
            M(dve.memset(top[:, :, TOPK:], -1.0), "top four", "dve")
            W(dve, "top four")
            alone(dve)
            for t in range(NT):
                m = dve.match_replace(rest[:, t, :], top[:, t, :], px[:, t, :], 0.0)
            M(m, "rest", "dve")
            W(dve, "rest", "?gT mm")
            M(dve.tensor_tensor(gate[:, :, :], px[:, :, 0:NR0], rest[:, :, 0:NR0], ALU.subtract), "gate", "dve")
            yield
            i, used, ps = bank()
            j, used2, ps2 = bank()
            W(pe, "kv", "q sin cos", used, used2)
            for s in range(2):
                pe.matmul(ps, kvm[:, s, :], qs[:, s, :], start=(s == 0), stop=(s == 1))
            for s in range(2):
                m = pe.matmul(ps2, dm[:, s, :], qs[:, s, :], start=(s == 0), stop=(s == 1))
            M(m, "attn mm", "pe")
            W(dve, "attn mm")
            M(dve.tensor_scalar(den[:, :], ps2, EPS_Z, None, ALU.max), "den", "dve")
            W(dve, "den")
            M(dve.reciprocal(den[:, :], den[:, :]), "rden", "dve")
            W(dve, "rden", "?downs")
            M(dve.tensor_tensor(at0[:, :], ps, den[:, :], ALU.mult), "attn", "dve")
            ring[1 + i] = "attn"
            ring[1 + j] = "attn"
            yield
        def second_part(b, par):
            xt = X[:, bass.ds(b * NT, NT), :]
            i, used, ps = bank()
            W(pe, "gate", used)
            for t in range(NT):
                m = pe.transpose(ps[0:NR0, t * P:(t + 1) * P], gate[:, t, :], ident)
            M(m, "gT mm", "pe")
            W(act, "gT mm", "?gate out", "?y mm")
            M(act.copy(gT[:, :], ps[0:NR0, :]), "gT", "act")
            ring[1 + i] = "gT"
            W(sp, "gT", "?gates")
            M(sp.dma_start(gate_d, gT[:, :]), "gate out", "gate out", 16)
            W(sp, "gate out", "attn mm", "r0 p")
            for i in range(2):
                src = gate_d.rearrange("(c i) l -> i c l", i=2)[i].unsqueeze(0).to_broadcast([ED, NC - 1, L])
                M(sp.dma_start(gates[i * ED:(i + 1) * ED, :, :], src), "gates", "gate in", 16)
            yield

            for c in range(NC):
                i, used, ps = bank()
                W(pe, used)
                M(pe.matmul(ps, up[:, c * P:(c + 1) * P], xnT[:, :], start=True, stop=True), f"up mm {c}", "pe")
                W(act, f"up mm {c}", "?downs")
                M(act.copy(hid[:, c, :], ps), f"up {c}", "act")
                ring[1 + i] = f"up {c}"
                yield
            for c in range(0, NC, 3):
                W(act, f"up {c + 2}")
                M(act.activation(hid[:, c:c + 3, :], hid[:, c:c + 3, :], ACT.Gelu), f"gelu {c // 3}", "act")
            yield
            i, used, acc = bank(hold=True)
            for c in range(NC):
                if c:
                    yield
                if c < NC - 1:
                    W(pool, f"gelu {(c + 1) // 3}", "gates")
                    M(pool.tensor_tensor(hid[:, c + 1, :], hid[:, c + 1, :], gates[:, c, :], ALU.mult),
                      f"gated {c + 1}" if c < NC - 2 else "gated all", "pool")
                W(pe, "gelu 0" if not c else f"gated {c}" if c < NC - 1 else "gated all", not c and used)
                pe.matmul(acc, down[:, c, :], hid[:, c, :], start=(c == 0), stop=False)
            M(pe.matmul(acc, wo[:, :], at0[:, :], start=False, stop=True), "downs", "pe")
            W(act, "downs", "?y mm")
            M(act.activation(yT[:, :], acc, ACT.Identity, bias=cols[:, 1:2]), "yT", "act")
            ring[1 + i], ring[3] = "yT", None
            yield
            i, ps = turn("y mm", lambda t: yT[:, t * P:(t + 1) * P], "yT")
            W(dve, "y mm")
            M(dve.tensor_tensor(xt, xt, ps.rearrange("p (t d) -> p t d", t=NT), ALU.add), "x1", "dve")
            ring[1 + i] = "x1"
            W(dve, "x1")

            yield from norm("1 ", xt, "0 xnT mm")
            i, ps = turn("1 xnT mm", lambda t: xn[:, t, :], "1 xn")
            W(act, "1 xnT mm", f"up mm {NC - 1}", "?v mm")
            act.copy(xh[:, :], ps)
            M(act.copy(xnT[:, :], ps), "xh", "act")
            W(dve, "xh")
            M(dve.tensor_tensor(xl[:, :], ps, xh[:, :], ALU.subtract), "xl", "dve")
            ring[1 + i] = "xl"
            yield

            i, used, ps = bank()
            W(pe, "xh", used)
            for t in range(NT):
                m = pe.matmul(ps[:, t * E1:(t + 1) * E1], xnT[:, t * P:(t + 1) * P], rw1[:, :], start=True, stop=True)
            M(m, "logits mm", "pe")
            W(dve, "logits mm")
            M(dve.tensor_tensor(lg1[:, :, :], ps[:, 0:NT * E1].rearrange("p (t e) -> p t e", t=NT),
                                rb1[:, :].unsqueeze(1).to_broadcast([P, NT, E1]), ALU.add), "logits", "dve")
            ring[1 + i] = "logits"
            yield
            for n in range(2):
                got = []
                for s in range(2):
                    i, used, ps = bank()
                    w = qk16[:, (2 * n + s) * D:(2 * n + s + 1) * D]
                    W(pe, "xl", used)
                    pe.matmul(ps, w, xh[:, :], start=True, stop=False)
                    m = pe.matmul(ps, w, xl[:, :], start=False, stop=True)
                    M(m, f"qk mm {n}{s}", "pe")
                    got.append((i, ps))
                W(dve, f"qk mm {n}0", "?low 1", "?low 0")
                dve.tensor_tensor(ra[:, :], got[0][1], k(K_RC), ALU.mult)
                W(dve, f"qk mm {n}1")
                M(dve.tensor_tensor(rb[:, :], got[1][1], k(K_RS), ALU.mult), f"rope {n}", "dve")
                for i, _ in got:
                    ring[1 + i] = f"rope {n}"
                W(pool, f"rope {n}", "?high 1", "?high 0")
                M(pool.tensor_tensor(ra[:, :], ra[:, :], rb[:, :], ALU.add), "rotated", "pool")
                yield
                W(act, "rotated", "?relayed out")
                M(act.copy(qkh[:, n, :], ra[:, :]), f"high {n}", "act")
                W(dve, f"high {n}", "?relayed out")
                M(dve.tensor_tensor(qkl[:, n, :], ra[:, :], qkh[:, n, :], ALU.subtract), f"low {n}", "dve")
                yield
            W(sp, "low 1", "?relayed in")
            for n, (name, order) in enumerate((("q", "hlhl"), ("k", "hllh"))):
                for c, part in enumerate(order):
                    src = qkh if part == "h" else qkl
                    M(sp.dma_start(relay[name][:, c], src[:, n, :]), "relayed out", "relay out", 16)
            W(sp, "relayed out", f"?scores {par}")
            M(sp.dma_start(qp[par][MROW:MROW + 2, :, :], qp[par][2 * MROW:2 * MROW + 2, :, :]),
              "relayed in", "relay in", 16)
            for name, dst in (("q", qp[par]), ("k", kp[par])):
                M(sp.dma_start(dst[0:MROW, :, :], relay[name].rearrange("h c d l -> (c d) h l")),
                  "relayed in", "relay in", 16)
            i, used, ps = bank()
            W(pe, "xl", used)
            for t in range(NT):
                o = ps[:, t * P:(t + 1) * P]
                pe.matmul(o, xh[:, t * P:(t + 1) * P], v16[:, :], start=True, stop=False)
                m = pe.matmul(o, xl[:, t * P:(t + 1) * P], v16[:, :], start=False, stop=True)
            M(m, "v mm", "pe")
            W(act, "v mm", f"?pv {par}")
            v = ps.rearrange("p (t h d) -> p t h d", t=NT, h=H)
            M(act.copy(vp[par][:, :, :, 0:HD], v), "v high", "act")
            W(dve, "v high", f"?pv {par}")
            M(dve.tensor_tensor(vp[par][:, :, :, HD + 1:], v, vp[par][:, :, :, 0:HD], ALU.subtract), f"v {par}", "dve")
            ring[1 + i] = f"v {par}"
            yield

            yield from softmax("r1 ", lg1[:, :, :], E1, e1[:, :, :], p1[:, :, :])
            pm = pmax[:, bass.ds(b * NT, NT)]
            dve.tensor_reduce(s1[:, 3, :], p1[:, :, :], AX_X, ALU.max)
            M(dve.tensor_reduce(pm, p1[:, :, :], AX_X, ALU.max), "p max", "dve")
            W(dve, "p max")
            desc = kc[:, int(KO[K_E]) + E1:int(KO[K_E]) + 2 * E1].unsqueeze(1).to_broadcast([P, NT, E1])
            M(dve.tensor_tensor(rk[:, :, :], p1[:, :, :], s1[:, 3, :].unsqueeze(2).to_broadcast([P, NT, E1]),
                                ALU.is_equal), "is max", "dve")
            W(dve, "is max")
            M(dve.tensor_tensor(rk[:, :, :], rk[:, :, :], desc, ALU.mult), "order", "dve")
            W(dve, "order")
            M(dve.tensor_reduce(s1[:, 4, :], rk[:, :, :], AX_X, ALU.max), "first", "dve")
            W(dve, "first", "?ranks mm")
            first = s1[:, 4, :].unsqueeze(2).to_broadcast([P, NT, E1])
            dve.tensor_tensor(ohb[:, :, :], first, desc, ALU.is_equal)
            M(dve.tensor_tensor(oh[:, :, :], first, desc, ALU.is_equal), "one hot", "dve")
            yield
            i, used, ps = bank()
            W(pe, "one hot", used)
            for t in range(NT + 1):
                o = ps[:, t * E1:(t + 1) * E1]
                for s in range(t):
                    m = pe.matmul(o, oneb[:, :], ohb[:, s, :], start=(s == 0), stop=(t == NT and s == NT - 1))
                if t < NT:
                    m = pe.matmul(o, trib[:, :], ohb[:, t, :], start=(t == 0), stop=True)
            M(m, "ranks mm", "pe")
            W(dve, "ranks mm")
            M(dve.tensor_tensor(rk[:, :, :], ps[:, 0:NT * E1].rearrange("p (t e) -> p t e", t=NT),
                                base[:, :].unsqueeze(1).to_broadcast([P, NT, E1]), ALU.add), "rows", "dve")
            W(dve, "rows")
            M(dve.tensor_tensor(base[:, :], base[:, :], ps[:, NT * E1:(NT + 1) * E1], ALU.add), "base", "dve")
            ring[1 + i] = "base"
            M(dve.tensor_tensor(rk[:, :, :], rk[:, :, :], oh[:, :, :], ALU.mult), "row of its", "dve")
            W(dve, "row of its")
            sl = slots[:, bass.ds(b * NT, NT)]
            M(dve.tensor_reduce(s1[:, 2, :], rk[:, :, :], AX_X, ALU.add), "slot", "dve")
            W(dve, "slot", "?sorted")
            dve.tensor_copy(sl, s1[:, 2, :])
            M(dve.tensor_copy(slotu[:, :], s1[:, 2, :]), "slots", "dve")
            W(pool, "slots")
            alone(pool)
            for t in range(NT):
                M(pool.indirect_dma_start(xs_d, bass.IndirectOffsetOnAxis(ap=slotu[:, t:t + 1], axis=0),
                                          xn[:, t, :], None), "sorted", "scatter", 16)
            yield

        S_UNITS = [((0, 1, 2, 3), 0), ((0, 1), 1), ((2, 3), 1)] + [((j,), t) for t in (2, 3) for j in range(4)]
        sring = [0]
        VW = 2 * HD + 1
        LOW_ON_POOL = (1, 3)

        def max_unit(par, g, n):
            heads, qt = S_UNITS[n]
            N = (qt + 1) * P
            i = sring[0]
            sring[0] ^= 1
            ps = PS[:, S0 + i, :]
            W(pe, f"?max bank {i}", n == 0 and "relayed in")
            for m, j in enumerate(heads):
                pe.matmul(ps[:, m * N:(m + 1) * N], qp[par][:, 4 * g + j, qt * P:(qt + 1) * P],
                          kp[par][:, 4 * g + j, 0:N], start=(m == 0), stop=False, skip_group_check=True)
            nh = len(heads)
            sc = ps[:, 0:nh * N].rearrange("p (j c) -> p j c", j=nh)
            m = pe.matmul(sc[:, :, qt * P:], identb[:, :], negb[:, :].unsqueeze(1).to_broadcast([P, nh, P]),
                          start=False, stop=True, skip_group_check=True)
            M(m, f"max mm {n}", "pe")
            W(dve, f"max mm {n}")
            M(dve.tensor_reduce(nm[:, g % 2, qt, heads[0]:heads[0] + nh], sc, AX_X, ALU.max, negate=True),
              f"max bank {i}", "dve")

        def max_parts(g):
            W(dve, f"?m mm {g % 2}", "max bank 0", "max bank 1")
            M(dve.tensor_scalar(mt[:, g % 2, :, :, 0], nm[:, g % 2, :, :], 1.0 / BIG, None, ALU.mult), "m high", "dve")
            W(dve, "m high")
            M(dve.scalar_tensor_tensor(out=mt[:, g % 2, :, :, 1], in0=mt[:, g % 2, :, :, 0], scalar=-BIG,
                                       in1=nm[:, g % 2, :, :], op0=ALU.mult, op1=ALU.add), "m low", "dve")

        def max_rows(par, g):
            i, used, ps = bank()
            ps = ps.bitcast(F16)
            W(pe, "m low", used)
            alone(pe)
            for t in range(NT):
                m = pe.transpose(ps[0:8, t * P:(t + 1) * P], mt[:, g % 2, t, :, :].rearrange("p a b -> p (a b)"),
                                 identh[:, :])
            M(m, f"m mm {g % 2}", "pe")
            W(act, f"m mm {g % 2}", f"?m in {g % 2}")
            M(act.copy(mrow[:, g % 2, :], ps[0:8, 0:L]), "m row", "act")
            ring[1 + i] = "m row"
            W(sp, "m row")
            for j in range(4):
                M(sp.dma_start(qp[par][MROW:MROW + 2, 4 * g + j, :], mrow[2 * j:2 * j + 2, g % 2, :]),
                  f"m in {g % 2}", f"m{g % 2}", 16)

        PAIR = [[(0, 0, 0)], [(0, 1, 0), (0, 3, 384)], [(1, 0, 0)], [(1, 1, 0), (1, 3, 384)], [(0, 2, 0), (1, 2, 256)]]
        NS = 5 * H // 2

        def score_slot(par, u):
            g = u // 10
            i = u % 2
            ps = PS[:, ST0 + i, :]
            W(pe, f"?exp {(u - 2) % 4}", u % 10 == 0 and f"m in {g % 2}")
            for j, kt, o in PAIR[u % 5]:
                h = u // 5 * 2 + j
                pe.matmul(ps[:, o:o + L - kt * P], kp[par][:, h, kt * P:(kt + 1) * P], qp[par][:, h, kt * P:],
                          start=(o == 0), stop=False, skip_group_check=True)
            step = PAIR[u % 5][-1][2]
            d = ps.rearrange("p (a c) -> p a c", c=P)
            d = d[:, 0:step // P + 1:step // P, :] if step else d[:, 0:1, :]
            n = 2 if step else 1
            m = pe.matmul(d, negb[:, :], identb[:, :].unsqueeze(1).to_broadcast([P, n, P]),
                          start=False, stop=True, skip_group_check=True)
            M(m, "st mm" if u < NS - 1 else f"scores {par}", "pe")
            W(act, "st mm" if u < NS - 1 else f"scores {par}", f"?p low {(u - 2) % 4}", f"?pv slot {u % 4}")
            act.activation(pt[:, u % 2, :], ps, ACT.Exp, scale=1.0 / SCALE)
            M(act.activation(ph[:, u % 4, :], ps, ACT.Exp, scale=1.0 / SCALE), f"exp {u % 4}", "act")
            e, n = (pool, "pool") if u % 5 in LOW_ON_POOL else (dve, "dve")
            W(e, f"exp {u % 4}", f"?pv slot {u % 4}")
            M(e.tensor_tensor(pl[:, u % 4, :], pt[:, u % 2, :], ph[:, u % 4, :], ALU.subtract), f"p low {u % 4}", n)

        def value_slot(par, u):
            g = u // 10
            W(pe, f"p low {u % 4}", u == 0 and f"v {par}", u % 10 == 0 and f"?heads {g % 2}")
            for j, kt, o in PAIR[u % 5]:
                h = u // 5 * 2 + j
                for qt in range(kt, NT):
                    at = (qt * 4 + h % 4) * VW
                    c = o + (qt - kt) * P
                    pe.matmul(PS[:, PV0 + g % 2, at:at + VW], ph[:, u % 4, c:c + P], vp[par][:, kt, h, :],
                              start=(u % 10 == 0 and qt == 0), stop=False, skip_group_check=True)
                    m = pe.matmul(PS[:, PV0 + g % 2, at:at + VW], pl[:, u % 4, c:c + P], vp[par][:, kt, h, :],
                                  start=False, stop=(kt == qt), skip_group_check=True)
            M(m, f"pv slot {u % 4}", "pe")
            if u == NS - 1:
                fl.events[f"pv {par}"] = fl.events[f"pv slot {u % 4}"]
                if fl.loop:
                    fl.seen[(fl.loop, f"pv {par}")] = fl.seen[(fl.loop, f"pv slot {u % 4}")]

        def heads_out(g):
            o = PS[:, PV0 + g % 2, 0:16 * VW].rearrange("p (t j c) -> p t j c", t=NT, j=4)
            W(dve, f"pv slot {(10 * g + 9) % 4}", f"?heads {(g + 1) % 2}", g == 0 and "?mT mm")
            M(dve.reciprocal(rsum[:, :, :], o[:, :, :, HD]), "r sum", "dve")
            W(dve, "r sum")
            r = rsum[:, :, :].unsqueeze(3).to_broadcast([P, NT, 4, HD])
            m = merged[:, :, 4 * g:4 * g + 4, :]
            dve.tensor_tensor(mlow[:, :, :, :], o[:, :, :, HD + 1:], r, ALU.mult)
            M(dve.tensor_tensor(m, o[:, :, :, 0:HD], r, ALU.mult), "products", "dve")
            W(dve, "products")
            M(dve.tensor_tensor(m, m, mlow[:, :, :, :], ALU.add), f"heads {g % 2}", "dve")

        def attention(b, par, following):
            xt = X[:, bass.ds(b * NT, NT), :]
            nxt = []
            for u in range(NS + 2):
                if u < NS:
                    if u % 10 == 0 and u < NS - 10:
                        nxt = [(par, u // 10 + 1, n) for n in range(len(S_UNITS))]
                    score_slot(par, u)
                if u == NS - 10 and following is not None:
                    nxt = [(following, 0, n) for n in range(len(S_UNITS))]
                if nxt:
                    max_unit(*nxt.pop(0))
                if u >= 2:
                    value_slot(par, u - 2)
                if nxt:
                    max_unit(*nxt.pop(0))
                if u < NS - 10 and u % 10 == 6:
                    max_parts(u // 10 + 1)
                if u < NS - 10 and u % 10 == 7:
                    max_rows(par, u // 10 + 1)
                if u == NS - 4 and following is not None:
                    max_parts(0)
                if u == NS - 3 and following is not None:
                    max_rows(following, 0)
                if u % 10 == 1 and u > 1:
                    heads_out(u // 10 - 1)
                yield
            i, ps = turn("mT mm", lambda t: merged[:, t, :, :].rearrange("p h d -> p (h d)"), f"heads {(G - 1) % 2}")
            W(act, "mT mm", "?out mm")
            M(act.copy(mT[:, :], ps), "mT", "act")
            ring[1 + i] = "mT"
            yield
            i, used, ps = bank()
            W(pe, "mT", used)
            for t in range(NT):
                m = pe.matmul(ps[:, t * P:(t + 1) * P], mT[:, t * P:(t + 1) * P], wo1[:, :], start=True, stop=True)
            M(m, "out mm", "pe")
            W(dve, "out mm")
            M(dve.tensor_tensor(xt, xt, ps.rearrange("p (t d) -> p t d", t=NT), ALU.add), "x2", "dve")
            ring[1 + i] = "x2"
            yield

        def together(main, *sides):
            sides = [[gen, steps, lo, hi, 0] for gen, steps, lo, hi in sides if gen]
            at = 0
            for _ in main:
                at += 1
                for s in sides:
                    gen, steps, lo, hi, done = s
                    while s[0] and s[4] * (hi - lo) < (at - lo) * steps:
                        if next(gen, "end") == "end":
                            s[0] = None
                            break
                        s[4] += 1
            for s in sides:
                for _ in s[0] or ():
                    s[4] += 1
                assert s[1] == s[4]

        def attend(b, par, more=2):
            together(attention(b, par, 1 - par if more else None),
                     (second_part(b + 1, 1 - par) if more else None, STEPS2, 0, CUT),
                     (first_part(b + 2) if more == 2 else None, STEPS1, CUT, NS + 4))

        STEPS1, STEPS2, CUT = 12, 32, 29

        for part in first_part(0), second_part(0, 0):
            for _ in part:
                pass
        W(dve, "all x")
        for _ in first_part(1):
            pass
        for n in range(len(S_UNITS)):
            max_unit(0, 0, n)
        max_parts(0)
        max_rows(0, 0)
        engines = ("pe", "act", "dve", "pool")
        dmas = ("rest in", "gate out", "gate in", "relay out", "relay in", "m0", "m1", "scatter")
        for e in (pe, act, dve, pool, sp):
            fl.all(e, *engines, *dmas)
            alone(e)

        with nc.Fori(0, B // 2 - 1) as it:
            fl.enter("batches", it, B // 2 - 1)
            ring[:] = fl.plan.get("ring", ring)
            ring[0] = 0
            for par in range(2):
                attend(it * 2 + par, par)
            fl.seen["ring"] = list(ring)
            fl.leave()
        attend(B - 2, 0, 1)
        W(sp, "scores 0")
        M(sp.dma_start(w1, io["w1"]), "w1", "w1", 16)
        W(sp, "gated all", "q sin cos", "attn", "attn mm", "gate")
        M(sp.dma_start(w2[:, :], io["w2"]), "w1", "w1", 16)
        attend(B - 1, 1, 0)
        for e in (pe, act, dve, pool, sp):
            fl.all(e, *engines, *dmas)
            alone(e)

        where.pop().close()
        where.append(ctx.enter_context(ExitStack()))
        ti = sb("ti", [P, 4, E1 + 1], I32)
        tf = sb("tf", [P, 6, E1 + 1])
        yrow = sb("yrow", [P, B * NT])
        ystep = sb("ystep", [P, B * NT])
        ja = sb("ja", [P, E1 + 1, NTAB])
        jb = sb("jb", [P, E1 + 1, NTAB])
        jr = sb("jr", [P, 4, NTAB])
        ji = sb("ji", [P, 3, NTAB], I32)
        xsb = sb("xsb", [P, U, D])
        xsT = sb("xsT", [P, 2, P])
        sil = sb("sil", [P, 2, F1])
        act1 = sb("act1", [P, 2, F1])
        aT = sb("aT", [P, 2, F1])
        ysb = sb("ysb", [P, U, D])

        E = kc[:, int(KO[K_E]):int(KO[K_E]) + E1]
        idx9 = kc[:, int(KO[K_E]) + 2 * E1:int(KO[K_E + 1])]
        step = [0]

        def D_(ins):
            step[0] += 1
            M(ins, f"chain {step[0]}", "dve")
            W(dve, f"chain {step[0]}")

        M(dve.tensor_copy(ti[:, 0, 0:E1], base[:, :]), "zero rows", "dve")
        D_(dve.tensor_tensor(tf[:, 0, 0:E1], base[:, :], E, ALU.subtract))
        D_(dve.tensor_scalar(tf[:, 0, 0:E1], tf[:, 0, 0:E1], float(P - 1), None, ALU.add))
        D_(dve.tensor_copy(ti[:, 1, 0:E1], tf[:, 0, 0:E1]))
        D_(dve.tensor_scalar(ti[:, 2, 0:E1], ti[:, 1, 0:E1], 7, None, ALU.arith_shift_right))
        D_(dve.tensor_copy(tf[:, 1, 0:E1], ti[:, 2, 0:E1]))
        D_(dve.memset(tf[:, 2, 0:1], 0.0))
        for e in range(E1):
            D_(dve.tensor_tensor(tf[:, 2, e + 1:e + 2], tf[:, 2, e:e + 1], tf[:, 1, e:e + 1], ALU.add))
        D_(dve.memset(tf[:, 3, :], 1e9))
        D_(dve.tensor_copy(tf[:, 3, 0:E1], tf[:, 2, 1:E1 + 1]))
        jj = k(K_J).unsqueeze(1).to_broadcast([P, E1 + 1, NTAB])

        def over_j(v):
            return v.unsqueeze(2).to_broadcast([P, E1 + 1, NTAB])

        D_(dve.tensor_tensor(ja[:, :, :], jj, over_j(tf[:, 2, :]), ALU.is_ge))
        D_(dve.tensor_tensor(jb[:, :, :], jj, over_j(tf[:, 3, :]), ALU.is_lt))
        D_(dve.tensor_tensor(ja[:, :, :], ja[:, :, :], jb[:, :, :], ALU.mult))
        by_j = ja[:, :, :].rearrange("p e j -> p j e")
        D_(dve.tensor_tensor(jb[:, :, :], ja[:, :, :], over_j(idx9), ALU.mult))
        D_(dve.tensor_reduce(jr[:, 0, :], jb[:, :, :].rearrange("p e j -> p j e"), AX_X, ALU.add))
        D_(dve.tensor_tensor(jb[:, :, :], ja[:, :, :], over_j(tf[:, 2, :]), ALU.mult))
        D_(dve.tensor_reduce(jr[:, 1, :], jb[:, :, :].rearrange("p e j -> p j e"), AX_X, ALU.add))
        D_(dve.tensor_tensor(jr[:, 1, :], k(K_J), jr[:, 1, :], ALU.subtract))
        D_(dve.tensor_scalar(jr[:, 1, :], jr[:, 1, :], float(P), None, ALU.mult))
        D_(dve.scalar_tensor_tensor(out=jr[:, 2, :], in0=jr[:, 0, :], scalar=float(CAP), in1=jr[:, 1, :],
                                    op0=ALU.mult, op1=ALU.add))
        D_(dve.tensor_scalar(jr[:, 3, :], jr[:, 2, :], float(E1 * CAP), None, ALU.min))
        D_(dve.tensor_scalar(jr[:, 0, :], jr[:, 0, :], float(E1 - 1), float(2 * F1), ALU.min, ALU.mult))
        D_(dve.tensor_copy(ji[:, 0, :], jr[:, 0, :]))
        D_(dve.tensor_scalar(ji[:, 1, :], ji[:, 0, :], 1, None, ALU.arith_shift_right))
        D_(dve.tensor_copy(ji[:, 2, :], jr[:, 3, :]))
        M(dve.memset(act1[:, :, :], 0.0), "tables", "dve")
        D_(dve.tensor_scalar(tf[:, 4, 0:E1], tf[:, 2, 0:E1], float(P), None, ALU.mult))
        D_(dve.tensor_tensor(tf[:, 4, 0:E1], tf[:, 4, 0:E1], E, ALU.subtract))
        D_(dve.tensor_scalar(yrow[:, :], slots[:, :], float(LAG * P), None, ALU.add))
        for e in range(1, E1):
            D_(dve.tensor_tensor(tf[:, 5, 0:1], tf[:, 4, e:e + 1], tf[:, 4, e - 1:e], ALU.subtract))
            D_(dve.tensor_scalar(ystep[:, :], slots[:, :], float(e * CAP), tf[:, 5, 0:1], ALU.is_ge, ALU.mult))
            D_(dve.tensor_tensor(yrow[:, :], yrow[:, :], ystep[:, :], ALU.add))
        M(pool.memset(aT[:, :, :], 0.0), "no aT", "pool")
        W(sp, "zero rows")
        for e in range(E1):
            row = sp.value_load(ti[0:1, 0, e:e + 1], min_val=0, max_val=E1 * CAP - P)
            M(sp.dma_start(xs_d[bass.ds(row, P), :], zeros[:, :]), "pad", "pad", 16)
        M(sp.dma_start(xs_d[E1 * CAP:E1 * CAP + P, :], zeros[:, :]), "pad", "pad", 16)
        W(sp, "pad", "tables")
        W(pe, "tables", "w1", "no aT")
        W(act, "tables", "no aT")

        HB, TB, XB, YB = 0, 4, 5, 6

        def load(u, col):
            W(sp, f"?xsT mm {u}")
            row = sp.value_load(ji[0:1, 2, bass.ds(col, 1)], min_val=0, max_val=E1 * CAP)
            M(sp.dma_start(xsb[:, u, :], xs_d[bass.ds(row, P), :]), f"xs in {u}", f"xs{u}", 16)

        def tile_turned(u):
            W(pe, f"xs in {u}", "?xsT")
            M(pe.transpose(PS[:, XB, 0:P], xsb[:, u, :], ident), f"xsT mm {u}", "pe")
            W(act, f"xsT mm {u}", f"?h mm {(u - 2) % U}")
            M(act.copy(xsT[:, u % 2, :], PS[:, XB, 0:P]), "xsT", "act")

        def hidden(u, off):
            W(pe, "xsT", f"?glu {(u - 2) % U}")
            for i in range(2):
                m = pe.matmul(PS[:, HB + 2 * (u % 2) + i, :], xsT[:, u % 2, :], w1[:, bass.ds(off + i * F1, F1)],
                              start=True, stop=True)
            M(m, f"h mm {u}", "pe")
            W(act, f"h mm {u}", f"?glu {(u - 2) % U}")
            M(act.activation(sil[:, u % 2, :], PS[:, HB + 2 * (u % 2), :], ACT.Silu), f"silu {u}", "act")
            W(dve, f"silu {u}", f"?aT mm {(u - 2) % U}")
            M(dve.tensor_tensor(act1[:, u % 2, :], sil[:, u % 2, :], PS[:, HB + 2 * (u % 2) + 1, :], ALU.mult),
              f"glu {u}", "dve")

        def hidden_turned(u):
            W(pe, f"?glu {u}", f"?aT {(u - 1) % U}")
            for c in range(FC):
                m = pe.transpose(PS[:, TB, c * P:(c + 1) * P], act1[:, u % 2, c * P:(c + 1) * P], ident)
            M(m, f"aT mm {u}", "pe")
            W(dve, f"aT mm {u}", f"?y mm {(u - 2) % U}")
            M(dve.tensor_copy(aT[:, u % 2, :], PS[:, TB, :]), f"aT {u}", "dve")

        def outputs(u, off, row):
            W(pe, f"?aT {u}", f"?y copy {(u - 2) % U}")
            for c in range(FC):
                m = pe.matmul(PS[:, YB + u % 2, 0:D], aT[:, u % 2, c * P:(c + 1) * P],
                              w2[:, bass.ds(off + c * D, D)], start=(c == 0), stop=(c == FC - 1))
            M(m, f"y mm {u}", "pe")
            W(act, f"y mm {u}", f"?ys out {u}")
            M(act.copy(ysb[:, u, :], PS[:, YB + u % 2, 0:D]), f"y copy {u}", "act")
            W(sp, f"y copy {u}")
            M(sp.dma_start(ys_d[bass.ds(row, P), :], ysb[:, u, :]), f"ys out {u}", f"ys{u}", 16)

        def offset(col, of):
            return pe.value_load(ji[0:1, of, bass.ds(col, 1)], min_val=0, max_val=(E1 - 1) * (2 * F1, FC * D)[of])

        for u in range(AHEAD):
            load(u, LAG + u)
        tile_turned(0)
        W(pe, "xsT")
        W(sp, "xsT mm 0")
        with nc.Fori(0, NTILE // U) as it:
            fl.enter("experts", it, NTILE // U)
            for u in range(U):
                n = it * U + u
                off = offset(n + LAG, 0)
                load(u, n + (LAG + AHEAD))
                hidden(u, off)
                tile_turned((u + 1) % U)
                hidden_turned((u - 1) % U)
                off2 = offset(n, 1)
                outputs((u - 2) % U, off2, n * P)
            fl.leave()
        hidden_turned(U - 1)
        for n in range(NTILE, NTILE + LAG):
            outputs((n - LAG) % U, offset(n, 1), n * P)

        W(pool, *(f"ys out {u}" for u in range(U)), f"chain {step[0]}")
        yg = sb("yg", [P, 2, NT, D])
        with nc.Fori(0, B // 2) as it:
            fl.enter("gather", it, B // 2)
            for i in range(2):
                W(pool, f"?final {i}")
                sl = sb(f"sl{i}", [P, NT], U32)
                M(pool.tensor_copy(sl[:, :], yrow[:, bass.ds(it * 2 * NT + i * NT, NT)]), f"slots {i}", "pool")
                W(pool, f"slots {i}")
                alone(pool)
                for t in range(NT):
                    M(pool.indirect_dma_start(yg[:, i, t, :], None, ys_d,
                                              bass.IndirectOffsetOnAxis(ap=sl[:, t:t + 1], axis=0)),
                      f"gathered {i}", f"gather{i}", 16)
                W(dve, f"gathered {i}")
                for t in range(NT):
                    c = it * 2 * NT + (i * NT + t)
                    xt1 = X[:, bass.ds(c, 1), :].rearrange("p a d -> p (a d)")
                    m = dve.scalar_tensor_tensor(out=xt1, in0=yg[:, i, t, :], scalar=pmax[:, bass.ds(c, 1)],
                                                 in1=xt1, op0=ALU.mult, op1=ALU.add)
                M(m, f"final {i}", "dve")
                W(sp, f"final {i}")
                M(sp.dma_start(out_d[:, bass.ds(it * 2 + i, 1)].rearrange("p b t d -> p (b t) d"),
                               X[:, bass.ds(it * 2 * NT + i * NT, NT), :]), "out", "out", 16)
            fl.leave()
        W(sp, "out")
    return fl.seen


SCALE = float(np.sqrt(np.float16(D)))

_INS = [("x", (B, L, D), "float32"), ("consts", (P, int(KO[-1])), "float32"), ("wkv", (P, KVW), "float32"),
        ("bkv", (P, KVW), "float32"), ("wq", (P, D), "float32"), ("wo", (P, D), "float32"),
        ("cols", (P, 2), "float32"), ("up", (P, NC * P), "float32"), ("down", (P, NC, D), "float32"),
        ("qk16", (P, 4 * D), "float16"), ("v16", (P, D), "float16"), ("o16", (P, D), "float16"),
        ("rw1", (P, E1), "float32"), ("rb1", (P, E1), "float32"),
        ("w1", (P, E1 * 2 * F1), "float32"), ("w2", (P, E1 * FC * D), "float32")]


def build(nc, plan):
    io = {n: nc.dram_tensor("in_" + n, list(s), mybir.dt.from_np(np.dtype(d)), kind="ExternalInput").ap()
          for n, s, d in _INS}
    io["out"] = nc.dram_tensor("out_y", [B, L, D], F32, kind="ExternalOutput").ap()
    return program(nc, io, plan)


def layouts(a):
    f = np.float32
    swap = np.arange(D) ^ 1
    t = lambda w: np.ascontiguousarray(w.T)
    up = np.concatenate([a["L0_ffn_shared_up"].reshape(-1, D), a["L0_ffn_routed_up"].reshape(-1, D)])
    dn = np.concatenate([a["L0_ffn_shared_down"], a["L0_ffn_routed_down"]])
    dn = dn.transpose(0, 2, 1).reshape(NC, P, D).transpose(1, 0, 2)
    rows = lambda v: np.broadcast_to(v[None, :], (P, v.size))
    return {
        "x": a["L0_attn_x"], "consts": constants(),
        "wkv": np.concatenate([a["L0_attn_Wk"].T, a["L0_attn_Wv"].T, np.zeros((D, 1), f), a["L0_ffn_router_w"].T], 1),
        "bkv": rows(np.concatenate([a["L0_attn_bk"], a["L0_attn_bv"], np.ones(1, f), np.zeros(NR0, f)])),
        "wq": t(a["L0_attn_Wq"]), "wo": t(a["L0_attn_Wo"]),
        "cols": np.stack([a["L0_attn_bq"], a["L0_attn_bo"]], 1), "up": t(up), "down": dn,
        "qk16": np.concatenate([a["L1_attn_qw"], a["L1_attn_qw"][:, swap], a["L1_attn_kw"], a["L1_attn_kw"][:, swap]], 1),
        "v16": a["L1_attn_vw"], "o16": a["L1_attn_ow"], "rw1": a["L1_ffn_router_w"], "rb1": rows(a["L1_ffn_router_b"]),
        "w1": a["L1_ffn_w1"].transpose(1, 0, 2).reshape(P, -1),
        "w2": a["L1_ffn_w2"].reshape(E1, FC, P, D).transpose(2, 0, 1, 3).reshape(P, -1),
    }


def kernel(**inputs):
    import concourse.bacc as _bacc
    from concourse.bass_utils import run_bass_kernel_spmd as _run

    plan = build(_bacc.Bacc("TRN2", target_bir_lowering=False, num_devices=1), {})
    nc = _bacc.Bacc("TRN2", target_bir_lowering=False, num_devices=1)
    assert build(nc, plan) == plan
    arrays = {"in_" + n: np.ascontiguousarray(v) for n, v in layouts({n: np.asarray(v) for n, v in inputs.items()}).items()}
    r = _run(nc, [arrays], core_ids=[0])
    return r.results[0]["out_y"]
```

```python
from contextlib import ExitStack

import numpy as np

import concourse.bass as bass
from concourse import mybir

ALU = mybir.AluOpType
ACT = mybir.ActivationFunctionType
F32 = mybir.dt.float32
F16 = mybir.dt.float16
BF16 = mybir.dt.bfloat16
I32 = mybir.dt.int32
U32 = mybir.dt.uint32
AX_X = mybir.AxisListType.X

P = 128
B, L, D = 16, 512, 128
NT = L // P
H, HD = 16, 8
G = H // 4
MROW = 4 * HD
NR0, TOPK, ED = 16, 4, 64
NC = 1 + NR0 * ED // P
KVW = 2 * D + 1 + NR0
E1, F1 = 8, 512
FC = F1 // P
CAP = B * L + P
NTILE = B * NT + E1
RING = 4
U = 4
LAG, AHEAD = 2, 4
NTAB = LAG + NTILE + AHEAD
EPS = 1e-5
EPS_Z = 1e-4
BIG = 256.0
NSENT = 4

K_ID, K_NEG, K_BD, K_TRI, K_ONE, K_SINB, K_COSB, K_RC, K_RS, K_SC, K_BH, K_T, K_E, K_J = range(14)
WIDTHS = [P, P, P, P, P, L, L, L, L, 2 * NT, H, NT, 3 * E1 + 1, NTAB]
KO = np.concatenate([[0], np.cumsum(WIDTHS)]).astype(int)


def constants():
    f = np.float32
    t = np.zeros((P, int(KO[-1])), f)

    def put(k, v):
        t[:, KO[k]:KO[k + 1]] = v

    i = np.arange(P)
    put(K_ID, np.eye(P))
    put(K_NEG, np.where(i[None, :] > i[:, None], -1e10, 0.0))
    put(K_BD, (i[:, None] // HD == i[None, :] // HD))
    put(K_BH, (i[:, None] // HD == np.arange(H)[None, :]))
    put(K_T, i[:, None] + P * np.arange(NT)[None, :])
    put(K_TRI, (i[:, None] < i[None, :]))
    put(K_ONE, 1.0)
    idx = (f(np.pi / 2) * np.arange(1, L + 1, dtype=f) / f(L)).astype(f)
    put(K_SINB, np.sin(idx).astype(f)[None, :])
    put(K_COSB, np.cos(idx).astype(f)[None, :])
    sc = np.stack([np.sin(idx).reshape(NT, P).T, np.cos(idx).reshape(NT, P).T], 1).astype(f)
    put(K_SC, sc.reshape(P, 2 * NT))
    inv = (f(1.0) / np.power(f(10000.0), np.arange(0, HD, 2, dtype=f) / f(HD))).astype(f)
    ang = (np.arange(L, dtype=f)[None, :] * inv[(i % HD) // 2][:, None]).astype(f)
    put(K_RC, np.cos(ang))
    put(K_RS, np.sin(ang) * np.where(i % 2 == 0, -1.0, 1.0)[:, None])
    put(K_E, np.concatenate([np.arange(E1) * CAP, E1 - np.arange(E1), np.arange(E1 + 1)])[None, :].astype(f))
    put(K_J, (np.arange(NTAB) - LAG)[None, :])
    return t


class Flow:

    def __init__(self, nc, plan):
        self.nc, self.plan, self.seen = nc, plan, {}
        self.base, self.n, self.sems, self.events = {}, {}, {}, {}
        self.loop, self.turn, self.turns = None, None, 1

    def sem(self, name, handle, credit):
        self.sems[name], self.base[name], self.n[name] = handle, credit, 0
        if credit:
            self.nc.sync.nop().then_inc(handle, credit)

    def mark(self, ins, name, sem, by=1):
        ins.then_inc(self.sems[sem], by)
        self.n[sem] += by
        self.events[name] = (sem, self.loop, self.base[sem] + self.n[sem])
        if self.loop:
            self.seen[(self.loop, name)] = (sem, self.n[sem])

    def same(self, name, other):
        self.events[name] = self.events[other]
        if self.loop:
            self.seen[(self.loop, name)] = self.seen[(self.loop, other)]

    def value(self, name):
        maybe, name = name.startswith("?"), name.lstrip("?")
        if self.loop:
            if name in self.events and self.events[name][1] == self.loop:
                return (*self.events[name][::2], True)
            if (self.loop, name) in self.plan:
                sem, k = self.plan[(self.loop, name)]
                return sem, self.base[sem] - self.plan[(self.loop, "total", sem)] + k, True
        if name not in self.events:
            assert not self.plan or maybe, name
            return None, 0, False
        return (*self.events[name][::2], False)

    def wait(self, eng, *names):
        most = {}
        for name in filter(None, names):
            sem, const, turns = self.value(name)
            if sem and (sem not in most or most[sem] < (turns, const)):
                most[sem] = turns, const
        for i, (sem, (turns, const)) in enumerate(most.items()):
            if i and eng is self.nc.sync:
                eng.sem_inc(self.junk, 1)
            step = self.plan.get((self.loop, "total", sem), 1)
            eng.wait_ge(self.sems[sem], self.turn * step + const if turns else const)

    def all(self, eng, *sems):
        for s in sems:
            eng.wait_ge(self.sems[s], self.base[s] + self.n[s])

    def enter(self, loop, turn, turns):
        for s in self.n:
            self.base[s] += self.n[s]
            self.n[s] = 0
        self.loop, self.turn, self.turns = loop, turn, turns

    def leave(self):
        for s in self.n:
            self.seen[(self.loop, "total", s)] = self.n[s]
            rest = (self.turns - 1) * self.n[s]
            self.events = {k: (es, None, v + rest) if es == s and lo == self.loop else (es, lo, v)
                           for k, (es, lo, v) in self.events.items()}
            self.base[s] += self.turns * self.n[s]
            self.n[s] = 0
        self.loop = None


def program(nc, io, plan):
    pe, act, dve, pool, sp = nc.tensor, nc.scalar, nc.vector, nc.gpsimd, nc.sync
    fl = Flow(nc, plan)
    ctx = ExitStack()
    with ctx:
        where = [ctx]

        def sb(name, shape, dt=F32):
            return where[-1].enter_context(nc.sbuf_tensor(name, shape, dt))

        def sem(name, credit=1024):
            fl.sem(name, ctx.enter_context(nc.semaphore("s_" + name)), credit)

        junk = ctx.enter_context(nc.semaphore("s_junk"))
        fl.junk = junk
        for s in ("pe", "act", "dve", "pool"):
            sem(s)
        for s in ("in", "rest in", "w", "w1", "gate out", "gate in", "relay q", "relay k", "relay in", "clear",
                  "m0", "m1", "pad", *(f"xs{u}" for u in range(U)), "out"):
            sem(s)
        for s in ("scatter", *(f"ys{u}" for u in range(U))):
            sem(s, 0)

        def alone(eng):
            eng.sem_inc(junk, 1)

        M, W = fl.mark, fl.wait

        X = sb("X", [P, B * NT, D])
        kc = sb("kc", [P, int(KO[-1])])
        base = sb("base", [P, E1])
        token = sb("token", [P, NT])
        pmax = sb("pmax", [P, B * NT])
        zeros = sb("zeros", [P, D + 1])

        def k(i):
            return kc[:, int(KO[i]):int(KO[i + 1])]

        ident = k(K_ID)
        even = sb("even", [P, 2, H, L], F16)
        w1 = even[:, :, :, :].rearrange("p s h l -> p (s h l)").bitcast(F32)
        share = sb("share", [P, (NC - 1) * L])
        w2 = share
        where.append(ctx.enter_context(ExitStack()))
        wq = sb("wq", [P, D])
        wkv = sb("wkv", [P, KVW])
        bkv = sb("bkv", [P, KVW])
        wo = sb("wo", [P, D])
        up = sb("up", [P, NC * P])
        down = sb("down", [P, NC, D])
        cols = sb("cols", [P, 2])
        qk16 = sb("qk16", [P, 4 * D], F16)
        v16 = sb("v16", [P, D], F16)
        o16 = sb("o16", [P, D], F16)
        wo1 = sb("wo1", [P, D])
        rw1 = sb("rw1", [P, E1])
        rb1 = sb("rb1", [P, E1])
        identb = sb("identb", [P, P], BF16)
        identh = sb("identh", [P, P], F16)
        negb = sb("negb", [P, P], BF16)
        trib = sb("trib", [P, P], BF16)
        oneb = sb("oneb", [P, P], BF16)
        neghalf = sb("neghalf", [P, NT])

        st = sb("st", [P, NT, 6])
        mv = sb("mv", [P, NT, 2])
        ve = sb("ve", [P, NT])
        rstd = sb("rstd", [P, NT])
        xn = sb("xn", [P, NT, D + 1])
        xnT = sb("xnT", [P, L])
        kvr = share[:, 0:NT * KVW].rearrange("p (t c) -> p t c", t=NT)
        ks = share[:, NT * KVW:NT * KVW + 2 * L].rearrange("p (t s d) -> p t s d", t=NT, s=2)
        qs = share[:, NT * KVW + 2 * L:NT * KVW + 4 * L].rearrange("p (s l) -> p s l", s=2)
        gates = share[:, :].rearrange("p (c l) -> p c l", c=NC - 1)
        ra = sb("ra", [P, L])
        qT = ra
        kvm = sb("kvm", [P, 2, D + H])
        den = sb("den", [P, NT, H])
        rden = sb("rden", [P, NT, H])
        parts = sb("parts", [P, 2, L], F16)
        at0 = parts[:, :, :].rearrange("p s l -> p (s l)").bitcast(F32).rearrange("p (t h d) -> p t h d", t=NT, h=H)
        at0T = sb("at0T", [P, L])
        sm = sb("sm", [P, 3, NT])
        e0 = sb("e0", [P, NT, NR0])
        px = sb("px", [P, NT, NR0 + NSENT])
        top = sb("top", [P, NT, 8])
        rest = sb("rest", [P, NT, NR0 + NSENT])
        gate = sb("gate", [P, NT, NR0])
        hid = sb("hid", [P, NC, L])
        yT = sb("yT", [P, L])
        gT = yT[0:NR0, :]
        xh, xl = parts[:, 0, :], parts[:, 1, :]
        rb = sb("rb", [P, L])
        qkh = sb("qkh", [P, 2, L], F16)
        qkl = sb("qkl", [P, 2, L], F16)
        lg1 = sb("lg1", [P, NT, E1])
        s1 = sb("s1", [P, 5, NT])
        e1 = sb("e1", [P, NT, E1])
        p1 = sb("p1", [P, NT, E1])
        oh = sb("oh", [P, NT, E1])
        ohb = sb("ohb", [P, NT, E1], BF16)
        rk = sb("rk", [P, NT, E1])
        slotu = sb("slotu", [P, NT], U32)

        qp = [even[:, 0], sb("qp1", [P, H, L], F16)]
        kp = [even[:, 1], sb("kp1", [P, H, L], F16)]
        vp = [sb(f"vp{i}", [P, NT, H, 2 * HD + 1], F16) for i in range(2)]
        nm = sb("nm", [P, 2, NT, 4])
        mt = sb("mt", [P, 2, NT, 2, 4], F16)
        mrow = sb("mrow", [8, 2, L], F16)
        pt = sb("pt", [P, RING, L])
        ph = sb("ph", [P, RING, L], F16)
        pl = sb("pl", [P, RING, L], F16)
        rsum = sb("rsum", [P, NT, 4])
        mlow = sb("mlow", [P, NT, 4, HD])
        merged = sb("merged", [P, NT, H, HD])
        mT = sb("mT", [P, L])

        PS = ctx.enter_context(nc.psum_tensor("PS", [P, 8, L], F32))
        PV0, WK0 = 4, 6

        x_d = io["x"].rearrange("b (t p) d -> p b t d", p=P)
        out_d = io["out"].rearrange("b (t p) d -> p b t d", p=P)
        relay = {n: nc.dram_tensor("relay_" + n, [2, H, HD, L], F16, kind="Internal").ap() for n in "qk"}
        gate_d = nc.dram_tensor("gate_rows", [NR0, L], F32, kind="Internal").ap()
        xs_d = nc.dram_tensor("xs", [(E1 + 1) * CAP, D + 1], F32, kind="Internal").ap()
        ys_d = nc.dram_tensor("ys", [B * L + (U + NTILE + 2) * P, D], F32, kind="Internal").ap()

        M(sp.dma_start(X[:, 0:NT, :], x_d[:, 0]), "x", "in", 16)
        for i, (dst, src) in enumerate((
                (kc[:, :], io["consts"]), (wkv[:, :], io["wkv"]), (bkv[:, :], io["bkv"]), (wq[:, :], io["wq"]),
                (wo[:, :], io["wo"]), (cols[:, :], io["cols"]), (up[:, :], io["up"]), (down[:, :, :], io["down"]),
                (qk16[:, :], io["qk16"]), (v16[:, :], io["v16"]), (o16[:, :], io["o16"]), (rw1[:, :], io["rw1"]),
                (rb1[:, :], io["rb1"]))):
            M((act if i % 2 else sp).dma_start(dst, src), "weights", "w", 16)
        M(sp.dma_start(X[:, NT:, :], x_d[:, 1:].rearrange("p b t d -> p (b t) d")), "all x", "rest in", 16)

        pool.memset(neghalf[:, :], -0.5)
        pool.memset(zeros[:, 0:D], 0.0)
        pool.memset(zeros[:, D:], -1.0)
        pool.memset(px[:, :, NR0:], -1.0)
        pool.memset(vp[0][:, :, :, HD:HD + 1], 1.0)
        M(pool.memset(vp[1][:, :, :, HD:HD + 1], 1.0), "fills", "pool")
        for i in range(2):
            M(dve.memset(kp[i][:, :, :].rearrange("p h l -> p (h l)").bitcast(F32), 0.0), "zeros", "dve")
            W(pool, "zeros", "ones 0" if i else "fills")
            M(pool.memset(kp[i][MROW:MROW + 2, :, :], BIG), f"ones {i}", "pool")
        for i in range(2):
            M(dve.memset(qp[i][:, :, :].rearrange("p h l -> p (h l)").bitcast(F32), 0.0), "zero queries", "dve")
        W(pool, "ones 1")
        alone(pool)
        for e in (pe, act):
            W(e, "weights")
        act.copy(identb[:, :], ident)
        act.copy(identh[:, :], ident)
        act.copy(negb[:, :], k(K_NEG))
        act.copy(trib[:, :], k(K_TRI))
        act.copy(oneb[:, :], k(K_ONE))
        M(act.copy(wo1[:, :], o16[:, :]), "casts", "act")
        W(pe, "casts")
        W(dve, "x", "fills")

        ring = [0, "?none", "?none", None]

        def bank(hold=False):
            i = 1 - ring[3] if ring[3] is not None else ring[0]
            ring[0] = 1 - i
            if hold:
                ring[3] = i
            return i, ring[1 + i], PS[:, WK0 + i, :]

        def norm(n, xt, *free):
            alone(dve)
            for t in range(NT):
                m = dve.bn_stats(st[:, t, :], xt[:, t, :])
            M(m, n + "stats", "dve")
            W(dve, n + "stats")
            alone(dve)
            for t in range(NT):
                m = dve.bn_aggr(mv[:, t, :], st[:, t, :])
            M(m, n + "mean", "dve")
            W(pool, n + "mean")
            alone(pool)
            M(pool.tensor_scalar(ve[:, :], mv[:, :, 1], EPS, None, ALU.add), n + "var", "pool")
            W(pool, n + "var")
            M(pool.tensor_tensor(rstd[:, :], ve[:, :], neghalf[:, :], ALU.pow), n + "rstd", "pool")
            yield 3
            W(dve, n + "rstd", *free)
            for t in range(NT):
                m = dve.tensor_scalar(xn[:, t, 0:D], xt[:, t, :], mv[:, t, 0:1], rstd[:, t:t + 1],
                                      ALU.subtract, ALU.mult)
            M(m, n + "xn", "dve")
            yield 2

        def softmax(n, src, width, ex, out):
            M(dve.tensor_reduce(sm[:, 0, :], src, AX_X, ALU.max), n + "mx", "dve")
            W(dve, n + "mx")
            M(dve.tensor_tensor(ex, src, sm[:, 0, :].unsqueeze(2).to_broadcast([P, NT, width]), ALU.subtract),
              n + "sub", "dve")
            W(act, n + "sub")
            M(act.activation(ex, ex, ACT.Exp), n + "exp", "act")
            yield 3
            W(dve, n + "exp")
            M(dve.tensor_reduce(sm[:, 1, :], ex, AX_X, ALU.add), n + "sum", "dve")
            W(dve, n + "sum")
            M(dve.reciprocal(sm[:, 2, :], sm[:, 1, :]), n + "rs", "dve")
            W(dve, n + "rs")
            M(dve.tensor_tensor(out, ex, sm[:, 2, :].unsqueeze(2).to_broadcast([P, NT, width]), ALU.mult),
              n + "p", "dve")
            W(dve, n + "p")

        def turn(n, src, free):
            i, used, ps = bank()
            W(pe, free, used)
            for t in range(NT):
                m = pe.transpose(ps[:, t * P:(t + 1) * P], src(t), ident)
            M(m, n, "pe")
            return i, ps

        def up_product(c):
            i, used, ps = bank()
            W(pe, used)
            M(pe.matmul(ps, up[:, c * P:(c + 1) * P], xnT[:, :], start=True, stop=True), f"up mm {c}", "pe")
            W(act, f"up mm {c}", "?downs")
            M(act.copy(hid[:, c, :], ps), f"up {c}", "act")
            ring[1 + i] = f"up {c}"

        def first_part(b):
            xt = X[:, bass.ds(b * NT, NT), :]
            yield from norm("0 ", xt, "?0 xnT mm", "?1 xnT mm", "?sorted")

            i, ps = turn("0 xnT mm", lambda t: xn[:, t, 0:D], "0 xn")
            W(act, "0 xnT mm", "?logits mm")
            M(act.copy(xnT[:, :], ps), "0 xnT", "act")
            ring[1 + i] = "0 xnT"
            yield 1.5

            for t in range(NT):
                i, used, ps = bank()
                W(pe, "0 xnT", used)
                M(pe.matmul(ps[:, 0:KVW], xnT[:, t * P:(t + 1) * P], wkv[:, :], start=True, stop=True),
                  f"kvr mm {t}", "pe")
                W(dve, f"kvr mm {t}", "?gated all")
                M(dve.tensor_tensor(kvr[:, t, :], ps[:, 0:KVW], bkv[:, :], ALU.add), f"kvr {t}", "dve")
                ring[1 + i] = f"kvr {t}"
                W(dve, f"kvr {t}")
                for s in range(2):
                    m = dve.tensor_scalar(ks[:, t, s, :], kvr[:, t, 0:D], 0.0,
                                          k(K_SC)[:, s * NT + t:s * NT + t + 1], ALU.max, ALU.mult)
                M(m, f"k sin cos {t}", "dve")
                yield 0.3
                up_product(t)
                yield 1.12

            i, used, ps = bank()
            W(pe, used)
            M(pe.matmul(ps, wq[:, :], xnT[:, :], start=True, stop=True), "q mm", "pe")
            W(act, "q mm", "?q sin cos", "?low 1")
            M(act.activation(qT[:, :], ps, ACT.Relu, bias=cols[:, 0:1]), "q", "act")
            ring[1 + i] = "q"
            W(pool, "q")
            pool.tensor_tensor(qs[:, 0, :], qT[:, :], k(K_SINB), ALU.mult)
            M(pool.tensor_tensor(qs[:, 1, :], qT[:, :], k(K_COSB), ALU.mult), "q sin cos", "pool")
            yield 0.3
            up_product(4)
            yield 0.8

            i, used, ps = bank()
            W(pe, f"k sin cos {NT - 1}", used)
            for s in range(2):
                for t in range(NT):
                    m = pe.matmul(ps[:, s * 256:s * 256 + D + 1], ks[:, t, s, :], kvr[:, t, D:2 * D + 1],
                                  start=(t == 0), stop=(t == NT - 1))
            M(m, "kv mm", "pe")
            W(dve, "kv mm", "?attn mm")
            for s in range(2):
                dve.tensor_tensor(kvm[:, s, 0:D], ps[:, s * 256:s * 256 + D], k(K_BD), ALU.mult)
                m = dve.tensor_scalar(kvm[:, s, D:], k(K_BH), ps[:, s * 256 + D:s * 256 + D + 1], None, ALU.mult)
            M(m, "kv", "dve")
            ring[1 + i] = "kv"
            yield 2
            up_product(5)
            yield 0.98
            yield from softmax("r0 ", kvr[:, :, 2 * D + 1:], NR0, e0[:, :, :], px[:, :, 0:NR0])
            alone(dve)
            for t in range(NT):
                m = dve.max(top[:, t, :], px[:, t, 0:NR0])
            M(m, "top", "dve")
            W(dve, "top")
            M(dve.memset(top[:, :, TOPK:], -1.0), "top four", "dve")
            W(dve, "top four")
            alone(dve)
            for t in range(NT):
                m = dve.match_replace(rest[:, t, :], top[:, t, :], px[:, t, :], 0.0)
            M(m, "rest", "dve")
            W(dve, "rest", "?gT mm")
            M(dve.tensor_tensor(gate[:, :, :], px[:, :, 0:NR0], rest[:, :, 0:NR0], ALU.subtract), "gate", "dve")
            up_product(6)
            yield 2
            got = [bank(), bank()]
            W(pe, "kv", "q sin cos", got[0][1], got[1][1])
            for t in range(NT):
                for s in range(2):
                    m = pe.matmul(got[t // 2][2][:, t % 2 * 256:t % 2 * 256 + D + H], qs[:, s, t * P:(t + 1) * P],
                                  kvm[:, s, :], start=(s == 0), stop=(s == 1))
            M(m, "attn mm", "pe")
            W(dve, "attn mm")
            for i in range(2):
                o = got[i][2].rearrange("p (t c) -> p t c", t=2)
                m = dve.tensor_scalar(den[:, 2 * i:2 * i + 2, :], o[:, :, D:D + H], EPS_Z, None, ALU.max)
            M(m, "den", "dve")
            W(dve, "den")
            M(dve.reciprocal(rden[:, :, :], den[:, :, :]), "rden", "dve")
            W(dve, "rden", "?at0T mm", "?v mm", "?xl")
            for i in range(2):
                o = got[i][2].rearrange("p (t c) -> p t c", t=2)[:, :, 0:D].rearrange("p t (h d) -> p t h d", h=H)
                r = rden[:, 2 * i:2 * i + 2, :].unsqueeze(3).to_broadcast([P, 2, H, HD])
                M(dve.tensor_tensor(at0[:, 2 * i:2 * i + 2, :, :], o, r, ALU.mult), "attn", "dve")
                ring[1 + got[i][0]] = "attn"
            up_product(7)
            yield 1
            i, used, ps = bank()
            W(pe, "gate", used)
            for t in range(NT):
                m = pe.transpose(ps[0:NR0, t * P:(t + 1) * P], gate[:, t, :], ident)
            M(m, "gT mm", "pe")
            W(act, "gT mm", "?gate out", "?y mm")
            M(act.copy(gT[:, :], ps[0:NR0, :]), "gT", "act")
            ring[1 + i] = "gT"
            W(sp, "gT", "?gates")
            M(sp.dma_start(gate_d, gT[:, :]), "gate out", "gate out", 16)
            W(sp, "gate out", "attn mm", "r0 p")
            for i in range(2):
                src = gate_d.rearrange("(c i) l -> i c l", i=2)[i].unsqueeze(0).to_broadcast([ED, NC - 1, L])
                M(sp.dma_start(gates[i * ED:(i + 1) * ED, :, :], src), "gates", "gate in", 16)
            yield 1.05

            i, ps = turn("at0T mm", lambda t: at0[:, t, :, :].rearrange("p h d -> p (h d)"), "attn")
            W(act, "at0T mm", "?downs")
            M(act.copy(at0T[:, :], ps), "at0T", "act")
            ring[1 + i] = "at0T"
            up_product(8)
            yield 1

        def second_part(b, par):
            xt = X[:, bass.ds(b * NT, NT), :]
            W(sp, f"?scores {par}")
            M(sp.dma_start(qp[par][MROW:MROW + 2, :, :], qp[par][2 * MROW:2 * MROW + 2, :, :]), "cleared", "clear", 16)
            for c in range(0, NC, 3):
                W(act, f"up {c + 2}")
                M(act.activation(hid[:, c:c + 3, :], hid[:, c:c + 3, :], ACT.Gelu), f"gelu {c // 3}", "act")
            for c in range(1, NC):
                W(pool, f"gelu {c // 3}", "gates")
                M(pool.tensor_tensor(hid[:, c, :], hid[:, c, :], gates[:, c - 1, :], ALU.mult),
                  f"gated {c}" if c < NC - 1 else "gated all", "pool")
            burst.append(BURST)
            yield 7
            i, used, acc = bank(hold=True)
            for c in range(NC):
                if c:
                    yield 1.3
                W(pe, not c and "at0T", "gelu 0" if not c else f"gated {c}" if c < NC - 1 else "gated all", not c and used)
                pe.matmul(acc, down[:, c, :], hid[:, c, :], start=(c == 0), stop=False)
            M(pe.matmul(acc, wo[:, :], at0T[:, :], start=False, stop=True), "downs", "pe")
            W(act, "downs", "?y mm")
            M(act.activation(yT[:, :], acc, ACT.Identity, bias=cols[:, 1:2]), "yT", "act")
            ring[1 + i], ring[3] = "yT", None
            yield 1.05
            i, ps = turn("y mm", lambda t: yT[:, t * P:(t + 1) * P], "yT")
            W(dve, "y mm")
            M(dve.tensor_tensor(xt, xt, ps.rearrange("p (t d) -> p t d", t=NT), ALU.add), "x1", "dve")
            ring[1 + i] = "x1"
            W(dve, "x1")

            yield from norm("1 ", xt, "0 xnT mm")
            i, ps = turn("1 xnT mm", lambda t: xn[:, t, 0:D], "1 xn")
            W(act, "1 xnT mm", f"up mm {NC - 1}", "?v mm", "at0T mm")
            act.copy(xh[:, :], ps)
            M(act.copy(xnT[:, :], ps), "xh", "act")
            W(dve, "xh")
            M(dve.tensor_tensor(xl[:, :], ps, xh[:, :], ALU.subtract), "xl", "dve")
            ring[1 + i] = "xl"
            yield 2.5

            i, used, ps = bank()
            W(pe, "xh", used)
            for t in range(NT):
                m = pe.matmul(ps[:, t * E1:(t + 1) * E1], xnT[:, t * P:(t + 1) * P], rw1[:, :], start=True, stop=True)
            M(m, "logits mm", "pe")
            W(dve, "logits mm")
            M(dve.tensor_tensor(lg1[:, :, :], ps[:, 0:NT * E1].rearrange("p (t e) -> p t e", t=NT),
                                rb1[:, :].unsqueeze(1).to_broadcast([P, NT, E1]), ALU.add), "logits", "dve")
            ring[1 + i] = "logits"
            yield 1
            for n in range(2):
                got = []
                for s in range(2):
                    i, used, ps = bank()
                    w = qk16[:, (2 * n + s) * D:(2 * n + s + 1) * D]
                    W(pe, "xl", used)
                    pe.matmul(ps, w, xh[:, :], start=True, stop=False)
                    m = pe.matmul(ps, w, xl[:, :], start=False, stop=True)
                    M(m, f"qk mm {n}{s}", "pe")
                    got.append((i, ps))
                W(dve, f"qk mm {n}0", "?low 1", "?low 0")
                dve.tensor_tensor(ra[:, :], got[0][1], k(K_RC), ALU.mult)
                W(dve, f"qk mm {n}1")
                M(dve.tensor_tensor(rb[:, :], got[1][1], k(K_RS), ALU.mult), f"rope {n}", "dve")
                for i, _ in got:
                    ring[1 + i] = f"rope {n}"
                W(pool, f"rope {n}", "?high 1", "?high 0")
                M(pool.tensor_tensor(ra[:, :], ra[:, :], rb[:, :], ALU.add), "rotated", "pool")
                yield 2.5
                W(act, "rotated", "?relay out k", "?relay out q")
                M(act.copy(qkh[:, n, :], ra[:, :]), f"high {n}", "act")
                W(dve, f"high {n}", "?relay out k", "?relay out q")
                M(dve.tensor_tensor(qkl[:, n, :], ra[:, :], qkh[:, n, :], ALU.subtract), f"low {n}", "dve")
                W(sp, f"low {n}", "?relayed in")
                for c, src in enumerate((qkh, qkl)):
                    M(sp.dma_start(relay["qk"[n]][c], src[:, n, :]), "relay out " + "qk"[n], "relay " + "qk"[n], 16)
                yield 1
            for n, name in enumerate("qk"):
                W(sp, f"relay out {name}")
                for c in range(4):
                    src = relay[name][(c // 2, c % 2)[n]].rearrange("h d l -> d h l")
                    M(sp.dma_start((qp, kp)[n][par][c * HD:(c + 1) * HD, :, :], src), "relayed in", "relay in", 16)
            i, used, ps = bank()
            W(pe, "xl", used)
            for t in range(NT):
                o = ps[:, t * P:(t + 1) * P]
                pe.matmul(o, xh[:, t * P:(t + 1) * P], v16[:, :], start=True, stop=False)
                m = pe.matmul(o, xl[:, t * P:(t + 1) * P], v16[:, :], start=False, stop=True)
            M(m, "v mm", "pe")
            W(act, "v mm", f"?pv {par}")
            v = ps.rearrange("p (t h d) -> p t h d", t=NT, h=H)
            M(act.copy(vp[par][:, :, :, 0:HD], v), "v high", "act")
            W(dve, "v high", f"?pv {par}")
            M(dve.tensor_tensor(vp[par][:, :, :, HD + 1:], v, vp[par][:, :, :, 0:HD], ALU.subtract), f"v {par}", "dve")
            ring[1 + i] = f"v {par}"
            yield 0.34

            yield from softmax("r1 ", lg1[:, :, :], E1, e1[:, :, :], p1[:, :, :])
            pm = pmax[:, bass.ds(b * NT, NT)]
            dve.tensor_reduce(s1[:, 3, :], p1[:, :, :], AX_X, ALU.max)
            M(dve.tensor_reduce(pm, p1[:, :, :], AX_X, ALU.max), "p max", "dve")
            W(dve, "p max")
            desc = kc[:, int(KO[K_E]) + E1:int(KO[K_E]) + 2 * E1].unsqueeze(1).to_broadcast([P, NT, E1])
            M(dve.tensor_tensor(rk[:, :, :], p1[:, :, :], s1[:, 3, :].unsqueeze(2).to_broadcast([P, NT, E1]),
                                ALU.is_equal), "is max", "dve")
            W(dve, "is max")
            M(dve.tensor_tensor(rk[:, :, :], rk[:, :, :], desc, ALU.mult), "order", "dve")
            W(dve, "order")
            M(dve.tensor_reduce(s1[:, 4, :], rk[:, :, :], AX_X, ALU.max), "first", "dve")
            W(dve, "first", "?ranks mm")
            first = s1[:, 4, :].unsqueeze(2).to_broadcast([P, NT, E1])
            dve.tensor_tensor(ohb[:, :, :], first, desc, ALU.is_equal)
            M(dve.tensor_tensor(oh[:, :, :], first, desc, ALU.is_equal), "one hot", "dve")
            yield 5
            i, used, ps = bank()
            W(pe, "one hot", used)
            for t in range(NT + 1):
                o = ps[:, t * E1:(t + 1) * E1]
                for s in range(t):
                    m = pe.matmul(o, oneb[:, :], ohb[:, s, :], start=(s == 0), stop=(t == NT and s == NT - 1))
                if t < NT:
                    m = pe.matmul(o, trib[:, :], ohb[:, t, :], start=(t == 0), stop=True)
            M(m, "ranks mm", "pe")
            W(dve, "ranks mm")
            M(dve.tensor_tensor(rk[:, :, :], ps[:, 0:NT * E1].rearrange("p (t e) -> p t e", t=NT),
                                base[:, :].unsqueeze(1).to_broadcast([P, NT, E1]), ALU.add), "rows", "dve")
            W(dve, "rows")
            M(dve.tensor_tensor(base[:, :], base[:, :], ps[:, NT * E1:(NT + 1) * E1], ALU.add), "base", "dve")
            ring[1 + i] = "base"
            M(dve.tensor_tensor(rk[:, :, :], rk[:, :, :], oh[:, :, :], ALU.mult), "row of its", "dve")
            W(dve, "row of its")
            M(dve.tensor_scalar(token[:, :], token[:, :], float(L), None, ALU.add), "token", "dve")
            M(dve.tensor_reduce(s1[:, 2, :], rk[:, :, :], AX_X, ALU.add), "slot", "dve")
            W(dve, "slot", "token", "?sorted")
            dve.tensor_copy(xn[:, :, D], token[:, :])
            M(dve.tensor_copy(slotu[:, :], s1[:, 2, :]), "slots", "dve")
            W(pool, "slots")
            alone(pool)
            for t in range(NT):
                M(pool.indirect_dma_start(xs_d, bass.IndirectOffsetOnAxis(ap=slotu[:, t:t + 1], axis=0),
                                          xn[:, t, :], None), "sorted", "scatter", 16)
                yield 1

        S_UNITS = [((0, 1, 2, 3), 0), ((0, 1), 1), ((2, 3), 1)] + [((j,), t) for t in (2, 3) for j in range(4)]
        sring = [0]

        def score_bank():
            i = sring[0]
            sring[0] = (i + 1) % 4
            return i, PS[:, i, :]

        VW = 2 * HD + 1
        LOW_ON_POOL = (39,)

        def max_unit(par, g, n):
            heads, qt = S_UNITS[n]
            N = (qt + 1) * P
            i, ps = score_bank()
            W(pe, f"?bank {i}", n == 0 and "relayed in", n == 0 and "cleared")
            for m, j in enumerate(heads):
                pe.matmul(ps[:, m * N:(m + 1) * N], qp[par][:, 4 * g + j, qt * P:(qt + 1) * P],
                          kp[par][:, 4 * g + j, 0:N], start=(m == 0), stop=False, skip_group_check=True)
            nh = len(heads)
            sc = ps[:, 0:nh * N].rearrange("p (j c) -> p j c", j=nh)
            m = pe.matmul(sc[:, :, qt * P:], identb[:, :], negb[:, :].unsqueeze(1).to_broadcast([P, nh, P]),
                          start=False, stop=True, skip_group_check=True)
            M(m, f"max mm {n}", "pe")
            W(dve, f"max mm {n}")
            M(dve.tensor_reduce(nm[:, g % 2, qt, heads[0]:heads[0] + nh], sc, AX_X, ALU.max, negate=True),
              f"bank {i}", "dve")
            fl.same("max", f"bank {i}")

        def max_parts(g):
            W(dve, f"?m mm {g % 2}", "max")
            M(dve.tensor_scalar(mt[:, g % 2, :, 0, :], nm[:, g % 2, :, :], 1.0 / BIG, None, ALU.mult), "m high", "dve")
            W(dve, "m high")
            M(dve.scalar_tensor_tensor(out=mt[:, g % 2, :, 1, :], in0=nm[:, g % 2, :, :], scalar=1.0 / BIG,
                                       in1=mt[:, g % 2, :, 0, :], op0=ALU.mult, op1=ALU.subtract), "m low", "dve")

        def max_rows(par, g):
            i, used, ps = bank()
            ps = ps.bitcast(F16)
            W(pe, "m low", used)
            alone(pe)
            for t in range(NT):
                m = pe.transpose(ps[0:8, t * P:(t + 1) * P], mt[:, g % 2, t, :, :].rearrange("p a b -> p (a b)"),
                                 identh[:, :])
            M(m, f"m mm {g % 2}", "pe")
            W(act, f"m mm {g % 2}", f"?m in {g % 2}")
            M(act.copy(mrow[:, g % 2, :], ps[0:8, 0:L]), "m row", "act")
            ring[1 + i] = "m row"
            W(act, "m row")
            for c in range(2):
                M(act.dma_start(qp[par][MROW + c:MROW + c + 1, 4 * g:4 * g + 4, :], mrow[4 * c:4 * c + 4, g % 2, :]),
                  f"m in {g % 2}", f"m{g % 2}", 16)

        PAIR = [[(0, 0, 0)], [(0, 1, 0), (0, 3, 384)], [(1, 0, 0)], [(1, 1, 0), (1, 3, 384)], [(0, 2, 0), (1, 2, 256)]]
        NS = 5 * H // 2

        def score_slot(par, u):
            g = u // 10
            i, ps = score_bank()
            W(pe, f"?bank {i}", u % 10 == 0 and f"m in {g % 2}")
            for j, kt, o in PAIR[u % 5]:
                h = u // 5 * 2 + j
                pe.matmul(ps[:, o:o + L - kt * P], kp[par][:, h, kt * P:(kt + 1) * P], qp[par][:, h, kt * P:],
                          start=(o == 0), stop=False, skip_group_check=True)
            step = PAIR[u % 5][-1][2]
            d = ps.rearrange("p (a c) -> p a c", c=P)
            d = d[:, 0:step // P + 1:step // P, :] if step else d[:, 0:1, :]
            n = 2 if step else 1
            m = pe.matmul(d, negb[:, :], identb[:, :].unsqueeze(1).to_broadcast([P, n, P]),
                          start=False, stop=True, skip_group_check=True)
            M(m, "st mm" if u < NS - 1 else f"scores {par}", "pe")
            W(act, "st mm" if u < NS - 1 else f"scores {par}", f"?p low {(u - RING) % 4}", f"?pv slot {u % RING}")
            act.activation(pt[:, u % RING, :], ps, ACT.Exp, scale=1.0 / SCALE)
            M(act.activation(ph[:, u % RING, :], ps, ACT.Exp, scale=1.0 / SCALE), f"exp {u % RING}", "act")
            fl.same(f"bank {i}", f"exp {u % RING}")
            e, n = (pool, "pool") if u in LOW_ON_POOL else (dve, "dve")
            W(e, f"exp {u % RING}", f"?pv slot {u % RING}")
            M(e.tensor_tensor(pl[:, u % RING, :], pt[:, u % RING, :], ph[:, u % RING, :], ALU.subtract), f"p low {u % RING}", n)

        def value_slot(par, u):
            g = u // 10
            W(pe, f"p low {u % RING}", u == 0 and f"v {par}", u % 10 == 0 and f"?heads {g % 2}")
            for j, kt, o in PAIR[u % 5]:
                h = u // 5 * 2 + j
                for qt in range(kt, NT):
                    at = (qt * 4 + h % 4) * VW
                    c = o + (qt - kt) * P
                    pe.matmul(PS[:, PV0 + g % 2, at:at + VW], ph[:, u % RING, c:c + P], vp[par][:, kt, h, :],
                              start=(u % 10 == 0 and qt == 0), stop=False, skip_group_check=True)
                    m = pe.matmul(PS[:, PV0 + g % 2, at:at + VW], pl[:, u % RING, c:c + P], vp[par][:, kt, h, :],
                                  start=False, stop=(kt == qt), skip_group_check=True)
            M(m, f"pv slot {u % RING}", "pe")
            if u == NS - 1:
                fl.same(f"pv {par}", f"pv slot {u % RING}")

        def heads_out(g):
            o = PS[:, PV0 + g % 2, 0:16 * VW].rearrange("p (t j c) -> p t j c", t=NT, j=4)
            W(dve, f"pv slot {(10 * g + 9) % RING}", f"?heads {(g + 1) % 2}", g == 0 and "?mT mm")
            M(dve.reciprocal(rsum[:, :, :], o[:, :, :, HD]), "r sum", "dve")
            W(dve, "r sum")
            r = rsum[:, :, :].unsqueeze(3).to_broadcast([P, NT, 4, HD])
            m = merged[:, :, 4 * g:4 * g + 4, :]
            dve.tensor_tensor(mlow[:, :, :, :], o[:, :, :, HD + 1:], r, ALU.mult)
            M(dve.tensor_tensor(m, o[:, :, :, 0:HD], r, ALU.mult), "products", "dve")
            W(dve, "products")
            M(dve.tensor_tensor(m, m, mlow[:, :, :, :], ALU.add), f"heads {g % 2}", "dve")

        burst, BURST = [], 10
        UNITS, PARTS, ROWS = (1, 1), (5, 6, 6, 6), (6, 7, 7, 7)
        TAIL = 1
        VLAG = 3

        def attention(b, par, following):
            xt = X[:, bass.ds(b * NT, NT), :]
            nxt = []
            for u in range(NS + VLAG):
                if VLAG <= u < NS:
                    score_slot(par, u)
                if u >= NS and following is not None:
                    score_slot(following, u - NS)
                if u % 10 == 0 and u < NS - 10:
                    nxt = [(par, u // 10 + 1, n) for n in range(len(S_UNITS))]
                if u == NS - 11 and following is not None:
                    nxt = [(following, 0, n) for n in range(len(S_UNITS))]
                for a in nxt[:UNITS[0]]:
                    max_unit(*a)
                del nxt[:UNITS[0]]
                yield
                if u >= VLAG:
                    value_slot(par, u - VLAG)
                n = UNITS[1] + (burst.pop() if burst else 0)
                for a in nxt[:n]:
                    max_unit(*a)
                del nxt[:n]
                if u < NS - 10 and u % 10 == PARTS[u // 10]:
                    max_parts(u // 10 + 1)
                if u < NS - 10 and u % 10 == ROWS[u // 10]:
                    max_rows(par, u // 10 + 1)
                if u == NS - 11 + PARTS[-1] and following is not None:
                    max_parts(0)
                if u == NS - 11 + ROWS[-1] and following is not None:
                    max_rows(following, 0)
                if u >= VLAG and (u - VLAG) % 10 == 9:
                    heads_out((u - VLAG) // 10)
                yield
            for _ in range(TAIL):
                yield
            i, ps = turn("mT mm", lambda t: merged[:, t, :, :].rearrange("p h d -> p (h d)"), f"heads {(G - 1) % 2}")
            W(act, "mT mm", "?out mm")
            M(act.copy(mT[:, :], ps), "mT", "act")
            ring[1 + i] = "mT"
            yield
            i, used, ps = bank()
            W(pe, "mT", used)
            for t in range(NT):
                m = pe.matmul(ps[:, t * P:(t + 1) * P], mT[:, t * P:(t + 1) * P], wo1[:, :], start=True, stop=True)
            M(m, "out mm", "pe")
            W(dve, "out mm")
            M(dve.tensor_tensor(xt, xt, ps.rearrange("p (t d) -> p t d", t=NT), ALU.add), "x2", "dve")
            ring[1 + i] = "x2"
            yield

        def together(main, *sides):
            sides = [[gen, total, lo, hi, 0] for gen, total, lo, hi in sides if gen]
            at = 0
            for _ in main:
                at += 0.5
                for s in sides:
                    gen, total, lo, hi, done = s
                    while s[0] and s[4] * (hi - lo) < (at - lo) * total:
                        got = next(gen, None)
                        if got is None:
                            s[0] = None
                        else:
                            s[4] += got
            for s in sides:
                s[4] += sum(s[0] or ())
                assert abs(s[1] - s[4]) < 0.1, s[4]

        def attend(b, par, more=2):
            together(attention(b, par, 1 - par if more else None),
                     (second_part(b + 1, 1 - par) if more else None, WAIT2, FIRST2, CUT),
                     (first_part(b + 2) if more == 2 else None, WAIT1, CUT, LAST))

        WAIT1, WAIT2, CUT = 24.31, 46.29, 22
        LAST, FIRST2 = NS + VLAG + 1, 0

        part = first_part(0)
        next(part)
        W(dve, "weights", "fills")
        W(pool, "weights")
        dve.tensor_scalar(token[:, :], k(K_T), -float(L), None, ALU.add)
        M(dve.tensor_copy(base[:, :], kc[:, int(KO[K_E]):int(KO[K_E]) + E1]), "base", "dve")
        for _ in part:
            pass
        W(sp, "ones 1", "zero queries")
        for _ in second_part(0, 0):
            pass
        W(dve, "all x")
        for _ in first_part(1):
            pass
        for n in range(len(S_UNITS)):
            max_unit(0, 0, n)
        max_parts(0)
        max_rows(0, 0)
        for u in range(VLAG):
            score_slot(0, u)
        engines = ("pe", "act", "dve", "pool")
        dmas = ("rest in", "gate out", "gate in", "relay q", "relay k", "relay in", "clear", "m0", "m1", "scatter")
        for e in (pe, act, dve, pool, sp):
            fl.all(e, *engines, *dmas)
            alone(e)

        with nc.Fori(0, B // 2 - 1) as it:
            fl.enter("batches", it, B // 2 - 1)
            ring[:] = fl.plan.get("ring", ring)
            ring[0] = sring[0] = 0
            for par in range(2):
                attend(it * 2 + par, par)
            fl.seen["ring"] = list(ring)
            fl.leave()
        attend(B - 2, 0, 1)
        W(sp, "scores 0")
        M(sp.dma_start(w1, io["w1"]), "w1", "w1", 16)
        W(sp, "gated all", "q sin cos", "attn", "attn mm", "gate")
        M(sp.dma_start(w2[:, :], io["w2"]), "w1", "w1", 16)
        attend(B - 1, 1, 0)
        for e in (pe, act, dve, pool, sp):
            fl.all(e, *engines, *dmas)
            alone(e)

        where.pop().close()
        where.append(ctx.enter_context(ExitStack()))
        ti = sb("ti", [P, 4, E1 + 1], I32)
        tf = sb("tf", [P, 6, E1 + 1])
        spare = sb("spare", [P, 1])
        isno = sb("isno", [P, 1])
        rowu = sb("rowu", [P, U], U32)
        yg = sb("yg", [P, B * NT, D])
        ja = sb("ja", [P, E1 + 1, NTAB])
        jb = sb("jb", [P, E1 + 1, NTAB])
        jr = sb("jr", [P, 4, NTAB])
        ji = sb("ji", [P, 3, NTAB], I32)
        xsb = sb("xsb", [P, U, D + 1])
        xsT = sb("xsT", [P, 2, P])
        sil = sb("sil", [P, 2, F1])
        act1 = sb("act1", [P, 2, F1])
        aT = sb("aT", [P, 2, F1])
        ysb = sb("ysb", [P, U, D])

        E = kc[:, int(KO[K_E]):int(KO[K_E]) + E1]
        idx9 = kc[:, int(KO[K_E]) + 2 * E1:int(KO[K_E + 1])]
        step = [0]

        def D_(ins):
            step[0] += 1
            M(ins, f"chain {step[0]}", "dve")
            W(dve, f"chain {step[0]}")

        M(dve.tensor_copy(ti[:, 0, 0:E1], base[:, :]), "zero rows", "dve")
        D_(dve.tensor_tensor(tf[:, 0, 0:E1], base[:, :], E, ALU.subtract))
        D_(dve.tensor_scalar(tf[:, 0, 0:E1], tf[:, 0, 0:E1], float(P - 1), None, ALU.add))
        D_(dve.tensor_copy(ti[:, 1, 0:E1], tf[:, 0, 0:E1]))
        D_(dve.tensor_scalar(ti[:, 2, 0:E1], ti[:, 1, 0:E1], 7, None, ALU.arith_shift_right))
        D_(dve.tensor_copy(tf[:, 1, 0:E1], ti[:, 2, 0:E1]))
        D_(dve.memset(tf[:, 2, 0:1], 0.0))
        for e in range(E1):
            D_(dve.tensor_tensor(tf[:, 2, e + 1:e + 2], tf[:, 2, e:e + 1], tf[:, 1, e:e + 1], ALU.add))
        D_(dve.memset(tf[:, 3, :], 1e9))
        D_(dve.tensor_copy(tf[:, 3, 0:E1], tf[:, 2, 1:E1 + 1]))
        jj = k(K_J).unsqueeze(1).to_broadcast([P, E1 + 1, NTAB])

        def over_j(v):
            return v.unsqueeze(2).to_broadcast([P, E1 + 1, NTAB])

        D_(dve.tensor_tensor(ja[:, :, :], jj, over_j(tf[:, 2, :]), ALU.is_ge))
        D_(dve.tensor_tensor(jb[:, :, :], jj, over_j(tf[:, 3, :]), ALU.is_lt))
        D_(dve.tensor_tensor(ja[:, :, :], ja[:, :, :], jb[:, :, :], ALU.mult))
        D_(dve.tensor_tensor(jb[:, :, :], ja[:, :, :], over_j(idx9), ALU.mult))
        D_(dve.tensor_reduce(jr[:, 0, :], jb[:, :, :].rearrange("p e j -> p j e"), AX_X, ALU.add))
        D_(dve.tensor_tensor(jb[:, :, :], ja[:, :, :], over_j(tf[:, 2, :]), ALU.mult))
        D_(dve.tensor_reduce(jr[:, 1, :], jb[:, :, :].rearrange("p e j -> p j e"), AX_X, ALU.add))
        D_(dve.tensor_tensor(jr[:, 1, :], k(K_J), jr[:, 1, :], ALU.subtract))
        D_(dve.tensor_scalar(jr[:, 1, :], jr[:, 1, :], float(P), None, ALU.mult))
        D_(dve.scalar_tensor_tensor(out=jr[:, 2, :], in0=jr[:, 0, :], scalar=float(CAP), in1=jr[:, 1, :],
                                    op0=ALU.mult, op1=ALU.add))
        D_(dve.tensor_scalar(jr[:, 3, :], jr[:, 2, :], float(E1 * CAP), None, ALU.min))
        D_(dve.tensor_scalar(jr[:, 0, :], jr[:, 0, :], float(E1 - 1), float(2 * F1), ALU.min, ALU.mult))
        D_(dve.tensor_copy(ji[:, 0, :], jr[:, 0, :]))
        D_(dve.tensor_scalar(ji[:, 1, :], ji[:, 0, :], 1, None, ALU.arith_shift_right))
        D_(dve.tensor_copy(ji[:, 2, :], jr[:, 3, :]))
        M(dve.memset(act1[:, :, :], 0.0), "tables", "dve")
        M(pool.memset(aT[:, :, :], 0.0), "no aT", "pool")
        M(pool.tensor_scalar(spare[:, :], k(K_T)[:, 0:1], float(B * L + U * P + 1), None, ALU.add), "spare", "pool")
        M(pool.tensor_scalar(rowu[:, :], k(K_T), float(B * L), None, ALU.add), "spare rows", "pool")
        W(pool, "spare rows")
        alone(pool)
        for u in range(U):
            M(pool.indirect_dma_start(ys_d, bass.IndirectOffsetOnAxis(ap=rowu[:, u:u + 1], axis=0),
                                      zeros[:, 0:D], None), f"ys out {u}", f"ys{u}", 16)
        W(sp, "zero rows")
        for e in range(E1):
            row = sp.value_load(ti[0:1, 0, e:e + 1], min_val=0, max_val=E1 * CAP - P)
            M(sp.dma_start(xs_d[bass.ds(row, P), :], zeros[:, :]), "pad", "pad", 16)
        M(sp.dma_start(xs_d[E1 * CAP:E1 * CAP + P, :], zeros[:, :]), "pad", "pad", 16)
        W(sp, "pad", "tables")
        W(pe, "tables", "w1", "no aT")
        W(act, "tables", "no aT")

        HB, TB, XB, YB = 0, 4, 5, 6

        def load(u, col):
            W(sp, f"?xsT mm {u}", f"?rows {u}")
            row = sp.value_load(ji[0:1, 2, bass.ds(col, 1)], min_val=0, max_val=E1 * CAP)
            M(sp.dma_start(xsb[:, u, :], xs_d[bass.ds(row, P), :]), f"xs in {u}", f"xs{u}", 16)

        def tile_turned(u):
            W(pool, f"xs in {u}", f"?ys out {u}", "?next spare", "spare")
            alone(pool)
            M(pool.tensor_scalar(isno[:, :], xsb[:, u, D:D + 1], 0.0, spare[:, 0:1], ALU.is_lt, ALU.mult), "is no", "pool")
            W(pool, "is no")
            alone(pool)
            M(pool.tensor_scalar(rowu[:, u:u + 1], isno[:, :], xsb[:, u, D:D + 1], None, ALU.add), f"rows {u}", "pool")
            M(pool.tensor_scalar(spare[:, :], spare[:, :], float(P), None, ALU.add), "next spare", "pool")
            W(pe, f"xs in {u}", f"?xsT {(u - 1) % U}")
            M(pe.transpose(PS[:, XB, 0:P], xsb[:, u, 0:D], ident), f"xsT mm {u}", "pe")
            W(act, f"xsT mm {u}", f"?h mm {(u - 2) % U}")
            M(act.copy(xsT[:, u % 2, :], PS[:, XB, 0:P]), f"xsT {u}", "act")

        def hidden(u, off):
            W(pe, f"?xsT {u}", f"?glu {(u - 2) % U}")
            for i in range(2):
                m = pe.matmul(PS[:, HB + 2 * (u % 2) + i, :], xsT[:, u % 2, :], w1[:, bass.ds(off + i * F1, F1)],
                              start=True, stop=True)
            M(m, f"h mm {u}", "pe")
            W(act, f"h mm {u}", f"?glu {(u - 2) % U}")
            M(act.activation(sil[:, u % 2, :], PS[:, HB + 2 * (u % 2), :], ACT.Silu), f"silu {u}", "act")
            W(dve, f"silu {u}", f"?aT mm {(u - 2) % U}")
            M(dve.tensor_tensor(act1[:, u % 2, :], sil[:, u % 2, :], PS[:, HB + 2 * (u % 2) + 1, :], ALU.mult),
              f"glu {u}", "dve")

        def hidden_turned(u):
            W(pe, f"?glu {u}", f"?aT {(u - 1) % U}")
            for c in range(FC):
                m = pe.transpose(PS[:, TB, c * P:(c + 1) * P], act1[:, u % 2, c * P:(c + 1) * P], ident)
            M(m, f"aT mm {u}", "pe")
            W(dve, f"aT mm {u}", f"?y mm {(u - 2) % U}")
            M(dve.tensor_copy(aT[:, u % 2, :], PS[:, TB, :]), f"aT {u}", "dve")

        def outputs(u, off):
            W(pe, f"?aT {u}", f"?y copy {(u - 2) % U}")
            for c in range(FC):
                m = pe.matmul(PS[:, YB + u % 2, 0:D], aT[:, u % 2, c * P:(c + 1) * P],
                              w2[:, bass.ds(off + c * D, D)], start=(c == 0), stop=(c == FC - 1))
            M(m, f"y mm {u}", "pe")
            W(act, f"y mm {u}", f"?ys out {u}")
            M(act.copy(ysb[:, u, :], PS[:, YB + u % 2, 0:D]), f"y copy {u}", "act")
            W(pool, f"y copy {u}", f"?rows {u}")
            alone(pool)
            M(pool.indirect_dma_start(ys_d, bass.IndirectOffsetOnAxis(ap=rowu[:, u:u + 1], axis=0), ysb[:, u, :], None),
              f"ys out {u}", f"ys{u}", 16)

        def offset(col, of):
            return pe.value_load(ji[0:1, of, bass.ds(col, 1)], min_val=0, max_val=(E1 - 1) * (2 * F1, FC * D)[of])

        for u in range(AHEAD):
            load(u, LAG + u)
        tile_turned(0)
        W(pe, "xsT 0")
        W(sp, "xsT mm 0", "rows 0")
        with nc.Fori(0, NTILE // U) as it:
            fl.enter("experts", it, NTILE // U)
            for u in range(U):
                n = it * U + u
                off = offset(n + LAG, 0)
                load(u, n + (LAG + AHEAD))
                tile_turned((u + 1) % U)
                hidden(u, off)
                hidden_turned((u - 1) % U)
                off2 = offset(n, 1)
                outputs((u - LAG) % U, off2)
            fl.leave()
        hidden_turned(U - 1)
        for n in range(NTILE, NTILE + LAG):
            outputs((n - LAG) % U, offset(n, 1))

        W(sp, *(f"ys out {u}" for u in range(U)))
        Q = 4
        n = B * NT // Q
        for q in range(Q):
            src = ys_d[q * n * P:(q + 1) * n * P, :].rearrange("(t p) d -> p t d", p=P)
            M(sp.dma_start(yg[:, q * n:(q + 1) * n, :], src), f"y in {q}", f"xs{q}", 16)
        for q in range(Q):
            y, xq = yg[:, q * n:(q + 1) * n, :], X[:, q * n:(q + 1) * n, :]
            W(dve, f"y in {q}")
            M(dve.tensor_tensor(y, y, pmax[:, q * n:(q + 1) * n].unsqueeze(2).to_broadcast([P, n, D]), ALU.mult),
              "by p", "dve")
            W(dve, "by p")
            M(dve.tensor_tensor(xq, xq, y, ALU.add), f"final {q}", "dve")
            W(sp, f"final {q}")
            M(sp.dma_start(out_d[:, q * B // Q:(q + 1) * B // Q].rearrange("p b t d -> p (b t) d"), xq), "out", "out", 16)
        W(sp, "out")
    return fl.seen


SCALE = float(np.sqrt(np.float16(D)))

_INS = [("x", (B, L, D), "float32"), ("consts", (P, int(KO[-1])), "float32"), ("wkv", (P, KVW), "float32"),
        ("bkv", (P, KVW), "float32"), ("wq", (P, D), "float32"), ("wo", (P, D), "float32"),
        ("cols", (P, 2), "float32"), ("up", (P, NC * P), "float32"), ("down", (P, NC, D), "float32"),
        ("qk16", (P, 4 * D), "float16"), ("v16", (P, D), "float16"), ("o16", (P, D), "float16"),
        ("rw1", (P, E1), "float32"), ("rb1", (P, E1), "float32"),
        ("w1", (P, E1 * 2 * F1), "float32"), ("w2", (P, E1 * FC * D), "float32")]


def build(nc, plan):
    io = {n: nc.dram_tensor("in_" + n, list(s), mybir.dt.from_np(np.dtype(d)), kind="ExternalInput").ap()
          for n, s, d in _INS}
    io["out"] = nc.dram_tensor("out_y", [B, L, D], F32, kind="ExternalOutput").ap()
    return program(nc, io, plan)


def layouts(a):
    f = np.float32
    swap = np.arange(D) ^ 1
    t = lambda w: np.ascontiguousarray(w.T)
    up = np.concatenate([a["L0_ffn_shared_up"].reshape(-1, D), a["L0_ffn_routed_up"].reshape(-1, D)])
    dn = np.concatenate([a["L0_ffn_shared_down"], a["L0_ffn_routed_down"]])
    dn = dn.transpose(0, 2, 1).reshape(NC, P, D).transpose(1, 0, 2)
    rows = lambda v: np.broadcast_to(v[None, :], (P, v.size))
    return {
        "x": a["L0_attn_x"], "consts": constants(),
        "wkv": np.concatenate([a["L0_attn_Wk"].T, a["L0_attn_Wv"].T, np.zeros((D, 1), f), a["L0_ffn_router_w"].T], 1),
        "bkv": rows(np.concatenate([a["L0_attn_bk"], a["L0_attn_bv"], np.ones(1, f), np.zeros(NR0, f)])),
        "wq": t(a["L0_attn_Wq"]), "wo": t(a["L0_attn_Wo"]),
        "cols": np.stack([a["L0_attn_bq"], a["L0_attn_bo"]], 1), "up": t(up), "down": dn,
        "qk16": np.concatenate([a["L1_attn_qw"], a["L1_attn_qw"][:, swap], a["L1_attn_kw"], a["L1_attn_kw"][:, swap]], 1),
        "v16": a["L1_attn_vw"], "o16": a["L1_attn_ow"], "rw1": a["L1_ffn_router_w"], "rb1": rows(a["L1_ffn_router_b"]),
        "w1": a["L1_ffn_w1"].transpose(1, 0, 2).reshape(P, -1),
        "w2": a["L1_ffn_w2"].reshape(E1, FC, P, D).transpose(2, 0, 1, 3).reshape(P, -1),
    }


def kernel(**inputs):
    import concourse.bacc as _bacc
    from concourse.bass_utils import run_bass_kernel_spmd as _run

    plan = build(_bacc.Bacc("TRN2", target_bir_lowering=False, num_devices=1), {})
    nc = _bacc.Bacc("TRN2", target_bir_lowering=False, num_devices=1)
    assert build(nc, plan) == plan
    arrays = {"in_" + n: np.ascontiguousarray(v) for n, v in layouts({n: np.asarray(v) for n, v in inputs.items()}).items()}
    r = _run(nc, [arrays], core_ids=[0])
    return r.results[0]["out_y"]
```
